# Optimizing a Trainium2 kernel written in Bass

```python
import numpy as np
import jax
import jax.numpy as jnp

def _softmax(x, axis=-1):
    return jax.nn.softmax(x, axis=axis)

def _gelu(x):
    return jax.nn.gelu(x, approximate=True)

def _silu(x):
    return jax.nn.silu(x)

def _sigmoid(x):
    return jax.nn.sigmoid(x)

def _layernorm(x, axis=-1, eps=1e-05):
    m = jnp.mean(x, axis=axis, keepdims=True)
    v = jnp.var(x, axis=axis, keepdims=True)
    return (x - m) / jnp.sqrt(v + eps)

def _scatter_add(tgt, idx, src, axis=0):
    return tgt.at[idx].add(src)

def _segment_sum(src, seg, n):
    return jax.ops.segment_sum(src, seg, n)
kernel_name = 'mk_flamingo_gated_d1_seqx_r4_f3299b'

def setup_inputs(seed: int=0):
    np.random.seed(seed)
    _w = jnp.asarray

    def _rec_inputs():
        import jax
        import jax.numpy as jnp
        _rk = jax.random.key(seed)
        x = -0.0003929 + 0.9999 * jax.random.normal(jax.random.fold_in(_rk, 1), (16, 256, 256), jnp.float32)
        _lenS = 256 - jax.random.randint(jax.random.fold_in(_rk, 7), (16,), 0, max(1, 256 // 4) + 1, jnp.int32)
        _lenS2 = 256 - jax.random.randint(jax.random.fold_in(_rk, 8), (16,), 0, max(1, 256 // 4) + 1, jnp.int32)
        _ctx_1024P = jax.random.normal(jax.random.fold_in(_rk, 11), (16, 16, 256), jnp.float32)
        _ctx_1024c = jax.random.dirichlet(jax.random.fold_in(_rk, 511), 0.3 * jnp.ones((16,), jnp.float32), (16, 256))
        _ctx_1024t = jnp.einsum('bsk,bkd->bsd', _ctx_1024c, _ctx_1024P)
        _ctx_1024t = _ctx_1024t * jax.lax.rsqrt(jnp.mean(jnp.square(_ctx_1024t)) + 1e-12) * 0.953939
        ctx_1024 = 2.81802e-05 + 1.00001 * (_ctx_1024t + 0.3 * jax.random.normal(jax.random.fold_in(_rk, 611), (16, 256, 256), jnp.float32))
        _g = jax.random.normal(jax.random.fold_in(_rk, 9001), (2, 1), jnp.float32)
        _g = jnp.sign(_g) * jnp.maximum(jnp.abs(_g), 1.0) + (_g == 0) * 1.0
        g_xattn = _g[0]
        g_ffn = _g[1]
        return (x, ctx_1024, g_xattn, g_ffn)
    x, ctx_1024, g_xattn, g_ffn = _rec_inputs()

    def _L0_xattn_setup():
        import jax, jax.numpy as jnp
        import numpy as np
        key = jax.random.key(seed)
        ks = jax.random.split(key, 6)
        B, S, D, H = (4, 1024, 256, 16)
        q = jax.random.normal(ks[0], (B, S, D), dtype=jnp.float32)
        encoder_output = jax.random.normal(ks[1], (B, S, D), dtype=jnp.float32)
        W_kv = jax.random.normal(ks[2], (2 * D, D), dtype=jnp.float32) * 0.02
        b_kv = jax.random.normal(ks[3], (2 * D,), dtype=jnp.float32) * 0.02
        W_out = jax.random.normal(ks[4], (D, D), dtype=jnp.float32) * 0.02
        b_out = jax.random.normal(ks[5], (D,), dtype=jnp.float32) * 0.02
        return {'q': q, 'encoder_output': encoder_output, 'W_kv': W_kv, 'b_kv': b_kv, 'W_out': W_out, 'b_out': b_out, 'heads': H}
    _L0_xattn_all = _L0_xattn_setup()
    _L0_xattn_in = {k: v for k, v in _L0_xattn_all.items() if k in ('W_kv', 'b_kv', 'W_out', 'b_out')}
    del _L0_xattn_all

    def _L0_ffn_setup():
        import jax, jax.numpy as jnp
        import numpy as np
        NUM_EXPERTS = 8
        EXPERT_CAPACITY = 2.0
        DIM = 256
        HIDDEN_DIM = 1024
        key = jax.random.key(seed)
        k_x, k_g, k_w1, k_w2 = jax.random.split(key, 4)
        n, t, d, f, e = (8, 256, DIM, HIDDEN_DIM, NUM_EXPERTS)
        x = jax.random.normal(k_x, (n, t, d), dtype=jnp.float32)
        gate_w = jax.random.normal(k_g, (e, d), dtype=jnp.float32) * 0.02
        w1 = jax.random.normal(k_w1, (e, d, f), dtype=jnp.float32) * 0.02
        w2 = jax.random.normal(k_w2, (e, f, d), dtype=jnp.float32) * 0.02
        return {'x': x, 'gate_w': gate_w, 'w1': w1, 'w2': w2}
    _L0_ffn_all = _L0_ffn_setup()
    _L0_ffn_in = {k: v for k, v in _L0_ffn_all.items() if k in ('gate_w', 'w1', 'w2')}
    del _L0_ffn_all
    return {'x': x, 'ctx_1024': ctx_1024, 'g_xattn': g_xattn, 'g_ffn': g_ffn, 'L0_xattn_W_kv': _L0_xattn_in['W_kv'], 'L0_xattn_b_kv': _L0_xattn_in['b_kv'], 'L0_xattn_W_out': _L0_xattn_in['W_out'], 'L0_xattn_b_out': _L0_xattn_in['b_out'], 'L0_ffn_gate_w': _L0_ffn_in['gate_w'], 'L0_ffn_w1': _L0_ffn_in['w1'], 'L0_ffn_w2': _L0_ffn_in['w2']}

def reference(x, ctx_1024, g_xattn, g_ffn, L0_xattn_W_kv, L0_xattn_b_kv, L0_xattn_W_out, L0_xattn_b_out, L0_ffn_gate_w, L0_ffn_w1, L0_ffn_w2):
    import jax
    import jax.numpy as jnp

    def _L0_xattn_ref(q, encoder_output, W_kv, b_kv, W_out, b_out, heads):
        import jax, jax.numpy as jnp
        import numpy as np
        B, S, D = q.shape
        d_k = D // heads
        kv = (encoder_output @ W_kv.T + b_kv).reshape(B, S, heads, d_k, 2)
        k = kv[..., 0]
        v = kv[..., 1]
        qh = q.reshape(B, S, heads, d_k)
        scale = jnp.sqrt(jnp.float32(d_k))
        scores = jnp.einsum('bshd,bstd->bsht', qh, k) / scale
        attn = jax.nn.softmax(scores, axis=-1)
        context = jnp.einsum('bsht,bstd->bshd', attn, v).reshape(B, S, D)
        return context @ W_out.T + b_out

    def _L0_ffn_ref(x, gate_w, w1, w2):
        import jax, jax.numpy as jnp
        import numpy as np
        NUM_EXPERTS = 8
        EXPERT_CAPACITY = 2.0
        DIM = 256
        HIDDEN_DIM = 1024
        n, t, d = x.shape
        e = gate_w.shape[0]
        k = int(EXPERT_CAPACITY * t / e)
        scores = jnp.einsum('ntd,ed->nte', x, gate_w)
        probs = jax.nn.softmax(scores, axis=-1)
        g, m = jax.lax.top_k(probs.transpose(0, 2, 1), k)
        batch_idx = jnp.arange(n)[:, None, None]
        xin = x[batch_idx, m]
        h = jnp.einsum('nekd,edf->nekf', xin, w1)
        h = jax.nn.gelu(h, approximate=False)
        h = jnp.einsum('nekf,efd->nekd', h, w2)
        out_tok = g[..., None] * h
        out = jnp.zeros((n, t, d), dtype=x.dtype).at[batch_idx, m].add(out_tok)
        return out
    x = x + jnp.tanh(g_xattn[0]) * _L0_xattn_ref(_layernorm(x, axis=-1), ctx_1024, L0_xattn_W_kv, L0_xattn_b_kv, L0_xattn_W_out, L0_xattn_b_out, 16)
    x = x + jnp.tanh(g_ffn[0]) * _L0_ffn_ref(_layernorm(x, axis=-1), L0_ffn_gate_w, L0_ffn_w1, L0_ffn_w2)
    return x

_drawn_inputs = setup_inputs


def setup_inputs(seed=0):
    import zlib

    import numpy as np

    out = dict(_drawn_inputs(seed))
    spreads = {}
    factors = {'ctx_1024': 2.744,
     'L0_xattn_W_kv': 2.747,
     'L0_xattn_b_kv': 8.0,
     'L0_xattn_W_out': 2.691,
     'L0_xattn_b_out': 3.543,
     'L0_ffn_gate_w': 3.43,
     'L0_ffn_w1': 3.051,
     'L0_ffn_w2': 2.97}
    for name, (base, spread) in spreads.items():
        noise = np.random.default_rng([zlib.crc32(name.encode()), seed]).standard_normal(out[name].shape)
        drawn = base * np.exp(spread * noise) if base else spread * noise
        out[name] = jnp.asarray(drawn.astype(out[name].dtype))
    for name, factor in factors.items():
        out[name] = (out[name] * factor).astype(out[name].dtype)
    return out
```

```python
from contextlib import ExitStack

import concourse.bass as bass
from concourse import mybir


def flamingo_gated_block_kernel(nc, x, ctx_in, g_xattn, g_ffn, W_kv, b_kv, W_out, b_out, gate_w, w1, w2, out):
    fp32 = mybir.dt.float32
    bf16 = mybir.dt.bfloat16
    ALU = mybir.AluOpType
    ACT = mybir.ActivationFunctionType
    AX = mybir.AxisListType

    B, T, D = x.shape
    E, _, F = w1.shape
    P = 128
    H = 16
    DK = D // H
    CAP = 2 * T // E
    G = 4
    BG = B // G
    J = T // P
    TG = BG * J
    DC = D // P
    FC = F // P
    EP = E // 2
    HV = 11
    HP = H - HV
    NR = TG + 2
    EPS = 1e-5
    assert 2 * CAP == P and TG == E and BG == 4

    x_t = x.rearrange("b (j p) c -> (b j) p c", p=P)
    c_t = ctx_in.rearrange("b (j p) c -> (b j) p c", p=P)
    o_t = out.rearrange("b (j p) c -> (b j) p c", p=P)
    x2_d = nc.dram_tensor("x2_scratch", [B * J, P, D], fp32).ap()
    w1_d = w1.rearrange("e (c p) f -> e p c f", p=P)
    w2_d = w2.rearrange("e (f p) d -> e p f d", p=P)

    es = ExitStack()
    with es:
        def sb(name, shape, dt=fp32):
            return es.enter_context(nc.sbuf_tensor(name, shape, dt))

        def sem(name):
            return es.enter_context(nc.semaphore(name))

        def sems(name, k):
            return [sem(f"{name}{i}") for i in range(k)]

        ident = sb("ident", [P, P])
        iota1 = sb("iota1", [P, CAP])
        ones_f = sb("ones_f", [P, T])
        ones_b = sb("ones_b", [3, P], bf16)
        neg_half = sb("neg_half", [P, 2])
        tanh_g = sb("tanh_g", [P, 2])
        gates = sb("gates", [P, 2])
        wkvT = sb("wkvT", [P, DC, 2 * D])
        woT = sb("woT", [P, DC, D])
        gwT = sb("gwT", [P, DC, E])
        bias_row = sb("bias_row", [1, 3 * D])
        bias_pc = sb("bias_pc", [1, 3, 3 * D], bf16)
        bias_b = sb("bias_b", [3, 3 * D], bf16)
        wrow = sb("wrow", [P, 6, D])
        gwrow = sb("gwrow", [E, D])

        xt = sb("xt", [P, 4, D])
        ct = sb("ct", [P, 2, D])
        ctT = sb("ctT", [P, DC, P])
        q = sb("q", [P, 2, D])
        kvs = sb("kvs", [P, 2, 2 * D])
        prod_v = sb("prod_v", [P, HV * DK * DK])
        prod_p = sb("prod_p", [P, HP * DK * DK])
        tree_a = sb("tree_a", [P, HP * DK * 8])
        tree_b = sb("tree_b", [P, HP * DK * 4])
        tree_c = sb("tree_c", [P, HP * DK * 2])
        S = sb("S", [P, H * DK])
        Sc = sb("Sc", [P, H * DK])
        mx = sb("mx", [P, H])
        Ex = sb("Ex", [P, H * DK])
        den = sb("den", [P, H])
        rden = sb("rden", [P, H])
        co = sb("co", [P, D])
        con = sb("con", [P, D])
        coT = sb("coT", [P, DC, P])
        x2 = sb("x2", [P, 2, D])
        st1 = sb("st1", [P, 6])
        st2 = sb("st2", [P, 6])
        mv = sb("mv", [P, 2, 2])
        ve = sb("ve", [P, 2])
        rs = sb("rs", [P, 2])
        xn = sb("xn", [P, TG, D])
        xnT = sb("xnT", [P, DC, P])

        lg = sb("lg", [P, J, BG, E])
        lgs = sb("lgs", [P, J, BG, E])
        gmx = sb("gmx", [P, J * BG])
        pe_ = sb("pe_", [P, J, BG, E])
        gsum = sb("gsum", [P, J * BG])
        grec = sb("grec", [P, J * BG])
        pr = sb("pr", [P, J, BG, E])
        work = sb("work", [BG * E, T])
        top8 = sb("top8", [BG * E, 8])
        spare = sb("spare", [P, 1])
        mask = sb("mask", [BG * E, T])
        cum = sb("cum", [BG * E, T])
        posm = sb("posm", [P, T])
        posT = sb("posT", [P, J, BG, E])
        Sel = sb("Sel", [P, 2, J, E, CAP])
        Gs = sb("Gs", [P, J, E, CAP])

        xin = sb("xin", [P, DC, E, BG, CAP])
        GT = sb("GT", [P, BG, EP, T])
        w1s = sb("w1s", [P, 2, DC, F])
        w2s = sb("w2s", [P, 2, FC, D])
        hT = sb("hT", [P, FC, BG * CAP])
        ys = sb("ys", [P, 2, 2, D])
        Y = sb("Y", [P, BG, EP, D])
        xr = sb("xr", [P, 4, D])

        bank = [es.enter_context(nc.psum_tensor(f"bank{i}", [P, 512], fp32)) for i in range(8)]
        KV, S0, S1, HB, YB = bank[0:2], bank[2], bank[3], bank[4:6], bank[6:8]
        CB = HB + YB

        setup_loaded, setup_b, gates_tanh = sem("setup_loaded"), sem("setup_b"), sem("gates_tanh")
        ident_ready, consts_ready = sem("ident_ready"), sem("consts_ready")
        setup_t, setup_ev = sem("setup_t"), sem("setup_ev")
        bias_rows, bias_step, bias_moved = sem("bias_rows"), sem("bias_step"), sem("bias_moved")
        mv_set, grec_ready = sem("mv_set"), sem("grec_ready")
        x_loaded, c_loaded = sems("x_loaded", 4), sems("c_loaded", 2)
        ctT_psum, ctT_ready, kv_psum, kvs_ready = sem("ctT_psum"), sem("ctT_ready"), sem("kv_psum"), sem("kvs_ready")
        st_x, st_x2, mv_ready, ve_ready, rs_ready = sem("st_x"), sem("st_x2"), sem("mv_ready"), sem("ve_ready"), sem("rs_ready")
        q_ready, xn_ready = sem("q_ready"), sem("xn_ready")
        prodv_s, prodp_s, tree_s = sem("prodv_s"), sem("prodp_s"), sem("tree_s")
        Sv_done, Sp_done, mx_done, Sc_ready, E_ready, den_done, rden_done = (
            sem("Sv_done"), sem("Sp_done"), sem("mx_done"), sem("Sc_ready"), sem("E_ready"), sem("den_done"), sem("rden_done"))
        cov_done, cop_done, con_ready = sem("cov_done"), sem("cop_done"), sem("con_ready")
        coT_psum, coT_ready, wo_psum, x2_ready, x2_stored = (
            sem("coT_psum"), sem("coT_ready"), sem("wo_psum"), sem("x2_ready"), sems("x2_stored", 2))
        xnT_psum, xnT_ready, lg_psum, lg_ready = sem("xnT_psum"), sem("xnT_ready"), sem("lg_psum"), sem("lg_ready")
        gstep, gexp_ready, pr_ready, prT_psum, work_ready, found8, removed8, mask_ready, cum_ready, posm_ready = (
            sem("gstep"), sem("gexp_ready"), sem("pr_ready"), sem("prT_psum"), sem("work_ready"), sem("found8"),
            sem("removed8"), sem("mask_ready"), sem("cum_ready"), sem("posm_ready"))
        posT_psum, posT_ready, sel_ready, gs_ready = sem("posT_psum"), sem("posT_ready"), sem("sel_ready"), sem("gs_ready")
        gt_psum, gt_ready, xin_psum, xin_ready = sem("gt_psum"), sem("gt_ready"), sem("xin_psum"), sem("xin_ready")
        w1_loaded, w2_loaded = sems("w1_loaded", 2), sems("w2_loaded", 2)
        h_psum, h_ready, y_psum, y_ready = sem("h_psum"), sem("h_ready"), sem("y_psum"), sem("y_ready")
        y_moved = [sems("y_moved_even", 2), sems("y_moved_odd", 2)]
        comb_psum, fin_ready = sem("comb_psum"), sem("fin_ready")
        xr_loaded, out_stored = sems("xr_loaded", 4), sems("out_stored", 4)
        out_done = sem("out_done")

        block = es.enter_context(nc.Block())

        @block.sync
        def _(sp):
            def load_x(g, i):
                t = g * TG + i
                if not (isinstance(g, int) and g == 0 and i < 4):
                    sp.wait_ge(x2_ready, t - 3)
                sp.dma_start(xt[:, i % 4, :], x_t[bass.ds(t, 1)].rearrange("o p c -> p (o c)")).then_inc(x_loaded[i % 4], 16)

            def load_c(g, i):
                t = g * TG + i
                if not (isinstance(g, int) and g == 0 and i < 2):
                    sp.wait_ge(ctT_psum, t - 1)
                sp.dma_start(ct[:, i % 2, :], c_t[bass.ds(t, 1)].rearrange("o p c -> p (o c)")).then_inc(c_loaded[i % 2], 16)

            def store_x2(g, i, known=False):
                t = g * TG + i
                if not known:
                    sp.wait_ge(x2_ready, t + 1)
                sp.dma_start(x2_d[bass.ds(t, 1)].rearrange("o p c -> p (o c)"), x2[:, i % 2, :]).then_inc(x2_stored[i % 2], 16)

            def load_w1(g, e):
                if not (isinstance(g, int) and g == 0 and e < 2):
                    sp.wait_ge(h_psum, 4 * (g * E + e - 1))
                sp.dma_start(w1s[:, e % 2, :, :], w1_d[e % E]).then_inc(w1_loaded[e % 2], 16)

            def load_w2(g, e):
                if not (isinstance(g, int) and g == 0 and e < 2):
                    sp.wait_ge(y_psum, 2 * (g * E + e - 1))
                sp.dma_start(w2s[:, e % 2, :, :], w2_d[e % E]).then_inc(w2_loaded[e % 2], 16)

            def move_y(g, e):
                n = g * E + e
                sp.wait_ge(y_ready, 2 * n + 2)
                for beta in range(2):
                    rows = slice(CAP * (e % 2), CAP * (e % 2) + CAP)
                    sp.dma_start(Y[rows, beta:BG:2, e // 2, :], ys[CAP * beta:CAP * beta + CAP, e % 2, :, :]).then_inc(y_moved[e % 2][beta], 16)

            def finish(g):
                for i in range(TG):
                    t = g * TG + i
                    u = i % 4
                    if i >= 4:
                        sp.wait_ge(out_stored[u], 16 * (g + 1))
                    if i == 0 and isinstance(g, int):
                        for stored in x2_stored:
                            sp.wait_ge(stored, 16 * (TG // 2) * (g + 1))
                    sp.dma_start(xr[:, u, :], x2_d[bass.ds(t, 1)].rearrange("o p c -> p (o c)")).then_inc(xr_loaded[u], 16)
                    if i >= 3:
                        store_out(g, i - 3)
                for i in range(TG - 3, TG):
                    store_out(g, i)
                sp.wait_ge(out_done, 16 * (TG - 4) * (g + 1))

            def store_out(g, i):
                t = g * TG + i
                sp.wait_ge(fin_ready, t + 1)
                sp.dma_start(o_t[bass.ds(t, 1)].rearrange("o p c -> p (o c)"), xr[:, i % 4, :]).then_inc(out_stored[i] if i < 4 else out_done, 16)

            sp.dma_start(ct[:, 0, :], c_t[0]).then_inc(c_loaded[0], 16)
            for a in range(DC):
                rows = W_kv[2 * P * a:2 * P * (a + 1), :].rearrange("(n two) c -> two n c", two=2)
                for kv in range(2):
                    sp.dma_start(wrow[:, 2 * kv + a, :], rows[kv]).then_inc(setup_loaded, 16)
                sp.dma_start(wrow[:, 4 + a, :], W_out[P * a:P * (a + 1), :]).then_inc(setup_loaded, 16)
            sp.dma_start(gwrow[:, :], gate_w).then_inc(setup_loaded, 16)
            sp.dma_start(gates[:, 0:1], g_xattn.rearrange("(a n) -> a n", a=1).broadcast_to([P, 1])).then_inc(setup_b, 16)
            sp.dma_start(gates[:, 1:2], g_ffn.rearrange("(a n) -> a n", a=1).broadcast_to([P, 1])).then_inc(setup_b, 16)
            sp.dma_start(con[0:1, 0:D], b_kv.rearrange("(o a n) -> o a n", o=1, a=2)[:, 0, :]).then_inc(setup_b, 16)
            sp.dma_start(co[0:1, 0:D], b_kv.rearrange("(o a n) -> o a n", o=1, a=2)[:, 1, :]).then_inc(setup_b, 16)
            sp.dma_start(bias_row[0:1, 2 * D:3 * D], b_out.rearrange("(o n) -> o n", o=1)).then_inc(setup_b, 16)
            sp.dma_start(xt[:, 0, :], x_t[0]).then_inc(x_loaded[0], 16)
            load_x(0, 1)
            load_c(0, 1)
            sp.wait_ge(bias_step, 5)
            for k in range(3):
                sp.dma_start(bias_b[k:k + 1, :], bias_pc[0:1, k, :]).then_inc(bias_moved, 16)
            load_x(0, 2)
            for e in range(2):
                load_w1(0, e)
                load_w2(0, e)

            def slot_loads(g, i):
                if i + 3 < TG:
                    load_x(g, i + 3)
                if i + 2 < TG:
                    load_c(g, i + 2)

            for i in range(TG):
                slot_loads(0, i)
                if i > 0:
                    store_x2(0, i - 1)
            store_x2(0, TG - 1)
            with sp.Fori(0, G - 1) as g:
                for i in range(3):
                    load_x(g + 1, i)
                for i in range(2):
                    load_c(g + 1, i)
                for s in range(TG):
                    slot_loads(g + 1, s)
                    if s > 0:
                        store_x2(g + 1, s - 1)
                    load_w1(g, s + 2)
                    load_w2(g, s + 2)
                    move_y(g, s)
                finish(g)
                store_x2(g + 1, TG - 1, known=True)
            for s in range(E):
                if s + 2 < E:
                    load_w1(G - 1, s + 2)
                    load_w2(G - 1, s + 2)
                move_y(G - 1, s)
            finish(G - 1)
            for stored in x2_stored:
                sp.wait_ge(stored, 16 * B * J // 2)

        @block.gpsimd
        def _(pool):
            def share(in0, in1, dst, n_tree, done):
                pv = prod_p[:, :].rearrange("p (h a b) -> p h a b", a=DK, b=DK)
                pool.tensor_tensor(pv, in0, in1, ALU.mult).then_inc(prodp_s, 1)
                pool.wait_ge(prodp_s, n_tree + 1)
                src = prod_p[:, :].rearrange("p (r b) -> p r b", b=DK)
                for k, buf in enumerate((tree_a, tree_b, tree_c)):
                    w = DK >> (k + 1)
                    nxt = buf[:, :].rearrange("p (r b) -> p r b", b=w)
                    pool.tensor_tensor(nxt, src[:, :, 0:w], src[:, :, w:2 * w], ALU.add).then_inc(tree_s, 1)
                    pool.wait_ge(tree_s, 3 * n_tree + k + 1)
                    src = nxt
                pool.tensor_tensor(dst.rearrange("p (r b) -> p r b", b=1), src[:, :, 0:1], src[:, :, 1:2], ALU.add).then_inc(done, 1)

            def rsqrt(n):
                pool.wait_ge(ve_ready, n + 1)
                pool.tensor_tensor(rs[:, :], ve[:, :], neg_half[:, :], ALU.pow).then_inc(rs_ready, 1)

            def tile_of(g, i):
                t = g * TG + i
                qi = q[:, i % 2, :].rearrange("p (h d) -> p h d", d=DK)[:, HV:H, :]
                Kv = kvs[:, i % 2, 0:D].rearrange("p (t d) -> p t d", d=DK)
                Vv = kvs[:, i % 2, D:2 * D].rearrange("p (d t) -> p d t", t=DK)
                Ev = Ex[:, :].rearrange("p (h t) -> p h t", t=DK)[:, HV:H, :]
                full = [P, HP, DK, DK]
                pool.wait_ge(q_ready, t + 1)
                pool.wait_ge(kvs_ready, t + 1)
                if not (isinstance(g, int) and g == 0 and i == 0):
                    pool.wait_ge(Sc_ready, t)
                share(Kv.unsqueeze(1).broadcast_to(full), qi.unsqueeze(2).broadcast_to(full),
                      S[:, HV * DK:H * DK], 2 * t, Sp_done)
                rsqrt(NR * g + i + 1)
                pool.wait_ge(E_ready, t + 1)
                if not (isinstance(g, int) and g == 0 and i == 0):
                    pool.wait_ge(con_ready, t)
                share(Vv.unsqueeze(1).broadcast_to(full), Ev.unsqueeze(2).broadcast_to(full),
                      co[:, HV * DK:H * DK], 2 * t + 1, cop_done)

            def attention(g):
                rsqrt(NR * g)
                for i in range(TG):
                    tile_of(g, i)
                rsqrt(NR * g + TG + 1)

            def gated_selection(g):
                for b in range(BG):
                    n = g * BG + b
                    pool.wait_ge(sel_ready, n + 1)
                    if b > 0:
                        pool.wait_ge(gt_psum, J * n)
                    for j in range(J):
                        ins = pool.tensor_tensor(Gs[:, j], Sel[:, b % 2, j], pr[:, j, b, :].unsqueeze(2).broadcast_to([P, E, CAP]), ALU.mult)
                    ins.then_inc(gs_ready, 1)

            pool.iota(iota1[:, :], pattern=[[1, CAP]], base=1, channel_multiplier=0,
                      allow_small_or_imprecise_dtypes=True).then_inc(consts_ready, 1)
            pool.memset(neg_half[:, :], -0.5).then_inc(consts_ready, 1)
            pool.memset(ident[:, :], 0.0).then_inc(ident_ready, 1)
            pool.wait_ge(ident_ready, 1)
            pool.affine_select(out=ident[:, :], in_=ident[:, :], compare_op=ALU.not_equal, fill=1.0,
                               base=0, pattern=[[-1, P]], channel_multiplier=1).then_inc(ident_ready, 1)
            pool.wait_ge(consts_ready, 2)
            attention(0)
            with pool.Fori(0, G - 1) as g:
                gated_selection(g)
                attention(g + 1)
            gated_selection(G - 1)

        @block.vector
        def _(dve):
            def first(g, i=0):
                return isinstance(g, int) and g == 0 and i == 0

            def wait_apart(sem, value):
                dve.wait_ge(sem, value)
                dve.memset(spare[:, :], 0.0)

            def products(in0, in1, dst, n, done):
                pv = prod_v[:, :].rearrange("p (h a b) -> p h a b", a=DK, b=DK)
                dve.tensor_tensor(pv, in0, in1, ALU.mult).then_inc(prodv_s, 1)
                dve.wait_ge(prodv_s, n + 1)
                dve.tensor_reduce(dst, prod_v[:, :].rearrange("p (r b) -> p r b", b=DK), axis=AX.X, op=ALU.add).then_inc(done, 1)

            def stats(g, i_x, i_x2):
                if i_x is not None:
                    t = g * TG + i_x
                    dve.wait_ge(x_loaded[i_x % 4], 16 * (g * (TG // 4) + i_x // 4) + 16)
                    dve.bn_stats(st1[:, :], xt[:, i_x % 4, :]).then_inc(st_x, 1)
                    wait_apart(st_x, t + 1)
                    dve.bn_aggr(mv[:, 0, :], st1[:, :]).then_inc(mv_ready, 1)
                if i_x2 is not None:
                    t = g * TG + i_x2
                    dve.wait_ge(x2_ready, t + 1)
                    dve.bn_stats(st2[:, :], x2[:, i_x2 % 2, :]).then_inc(st_x2, 1)
                    wait_apart(st_x2, t + 1)
                    dve.bn_aggr(mv[:, 1, :], st2[:, :]).then_inc(mv_ready, 1)
                done = (TG if i_x is None else i_x + 1) + (0 if i_x2 is None else i_x2 + 1)
                dve.wait_ge(mv_ready, 2 * TG * g + done)
                dve.tensor_scalar(ve[:, :], mv[:, :, 1], EPS, None, ALU.add).then_inc(ve_ready, 1)

            def make_q(g, i):
                dve.tensor_scalar(q[:, i % 2, :], xt[:, i % 4, :], mv[:, 0, 0:1], rs[:, 0:1], ALU.subtract, ALU.mult).then_inc(q_ready, 1)

            def make_xn(g, i):
                if i == 0:
                    dve.wait_ge(xin_psum, DC * BG * g)
                dve.tensor_scalar(xn[:, i, :], x2[:, i % 2, :], mv[:, 1, 0:1], rs[:, 1:2], ALU.subtract, ALU.mult).then_inc(xn_ready, 1)

            def residual(g, i):
                t = g * TG + i
                dve.wait_ge(wo_psum, t + 1)
                if not (isinstance(g, int) and g == 0 and i < 2):
                    dve.wait_ge(x2_stored[i % 2], 16 * (g * (TG // 2) + i // 2))
                dve.scalar_tensor_tensor(x2[:, i % 2, :], S0[:, 0:D], tanh_g[:, 0:1], xt[:, i % 4, :],
                                         ALU.mult, ALU.add).then_inc(x2_ready, 1)

            def tile_of(g, i):
                t = g * TG + i
                full = [P, HV, DK, DK]
                kvp = KV[i % 2]
                Kp = kvp[:, 0:D].rearrange("p (t d) -> p t d", d=DK)
                Vp = kvp[:, D:2 * D].rearrange("p (d t) -> p d t", t=DK)
                qi = q[:, i % 2, :].rearrange("p (h d) -> p h d", d=DK)[:, 0:HV, :]
                Ev = Ex[:, :].rearrange("p (h t) -> p h t", t=DK)
                dve.wait_ge(kvs_ready, t + 1)
                dve.wait_ge(q_ready, t + 1)
                products(Kp.unsqueeze(1).broadcast_to(full), qi.unsqueeze(2).broadcast_to(full), S[:, 0:HV * DK], 2 * t, Sv_done)
                if i > 0:
                    residual(g, i - 1)
                stats(g, i + 1 if i + 1 < TG else None, i - 1 if i > 0 else None)
                dve.wait_ge(Sp_done, t + 1)
                dve.wait_ge(Sv_done, t + 1)
                Sv = S[:, :].rearrange("p (h t) -> p h t", t=DK)
                dve.reduce_max(mx[:, :], Sv, AX.X).then_inc(mx_done, 1)
                dve.wait_ge(mx_done, t + 1)
                if not first(g, i):
                    dve.wait_ge(E_ready, t)
                dve.tensor_tensor(Sc[:, :].rearrange("p (h t) -> p h t", t=DK), Sv,
                                  mx[:, :].unsqueeze(2).broadcast_to([P, H, DK]), ALU.subtract).then_inc(Sc_ready, 1)
                dve.wait_ge(rs_ready, NR * g + i + 2)
                if i + 1 < TG:
                    if not (isinstance(g, int) and g == 0 and i == 0):
                        dve.wait_ge(cop_done, t)
                    make_q(g, i + 1)
                if i > 0:
                    make_xn(g, i - 1)
                dve.wait_ge(E_ready, t + 1)
                dve.tensor_reduce(den[:, :], Ev, axis=AX.X, op=ALU.add).then_inc(den_done, 1)
                products(Vp.unsqueeze(1).broadcast_to(full), Ev[:, 0:HV, :].unsqueeze(2).broadcast_to(full), co[:, 0:HV * DK], 2 * t + 1, cov_done)
                dve.wait_ge(den_done, t + 1)
                dve.reciprocal(rden[:, :], den[:, :]).then_inc(rden_done, 1)
                dve.wait_ge(rden_done, t + 1)
                dve.wait_ge(cop_done, t + 1)
                dve.wait_ge(cov_done, t + 1)
                if not first(g, i):
                    dve.wait_ge(coT_psum, t)
                dve.tensor_tensor(con[:, :].rearrange("p (h d) -> p h d", d=DK), co[:, :].rearrange("p (h d) -> p h d", d=DK),
                                  rden[:, :].unsqueeze(2).broadcast_to([P, H, DK]), ALU.mult).then_inc(con_ready, 1)

            def begin_attention(g):
                stats(g, 0, None)
                dve.wait_ge(rs_ready, NR * g + 1)
                make_q(g, 0)

            def end_attention(g):
                residual(g, TG - 1)
                stats(g, None, TG - 1)
                dve.wait_ge(rs_ready, NR * g + NR)
                make_xn(g, TG - 1)

            def gate_softmax(g):
                v8 = lambda m: m[:, :, :, :].rearrange("p j b e -> p (j b) e")
                bc = lambda m: m[:, :].unsqueeze(2).broadcast_to([P, J * BG, E])
                dve.wait_ge(lg_ready, TG * g + TG)
                dve.reduce_max(gmx[:, :], v8(lg), AX.X).then_inc(gstep, 1)
                dve.wait_ge(gstep, 3 * g + 1)
                dve.tensor_tensor(v8(lgs), v8(lg), bc(gmx), ALU.subtract).then_inc(gstep, 1)
                dve.wait_ge(gexp_ready, g + 1)
                dve.reduce_sum(gsum[:, :], v8(pe_), AX.X).then_inc(gstep, 1)
                dve.wait_ge(gstep, 3 * g + 3)
                dve.reciprocal(grec[:, :], gsum[:, :]).then_inc(grec_ready, 1)
                dve.wait_ge(grec_ready, g + 1)
                dve.tensor_tensor(v8(pr), v8(pe_), bc(grec), ALU.mult).then_inc(pr_ready, 1)

            def choose_tokens(g):
                dve.wait_ge(prT_psum, g + 1)
                dve.tensor_copy(work[:, :], S1[0:BG * E, 0:T]).then_inc(work_ready, 1)
                wait_apart(work_ready, g + 1)
                for r in range(CAP // 8):
                    n = g * (CAP // 8) + r
                    dve.max(top8[:, :], work[:, :]).then_inc(found8, 1)
                    wait_apart(found8, n + 1)
                    dve.match_replace(work[:, :], top8[:, :], work[:, :], -1.0).then_inc(removed8, 1)
                    wait_apart(removed8, n + 1)
                dve.tensor_scalar(mask[:, :], work[:, :], 0.0, None, ALU.is_lt).then_inc(mask_ready, 1)
                dve.wait_ge(mask_ready, g + 1)
                dve.tensor_tensor_scan(cum[:, :], ones_f[0:BG * E, :], mask[:, :], 0.0, ALU.mult, ALU.add).then_inc(cum_ready, 1)
                dve.wait_ge(cum_ready, g + 1)
                dve.tensor_tensor(posm[0:BG * E, :], cum[:, :], mask[:, :], ALU.mult).then_inc(posm_ready, 1)

            def last_sums(g):
                for i in range(TG):
                    t = g * TG + i
                    dve.wait_ge(comb_psum, t + 1)
                    dve.wait_ge(xr_loaded[i % 4], 16 * (g * (TG // 4) + i // 4) + 16)
                    dve.scalar_tensor_tensor(xr[:, i % 4, :], CB[i % 4][:, 0:D], tanh_g[:, 1:2], xr[:, i % 4, :],
                                             ALU.mult, ALU.add).then_inc(fin_ready, 1)

            def selection(g):
                dve.wait_ge(posT_psum, g + 1)
                dve.tensor_copy(posT[:, :, :, :].rearrange("p j b e -> p j (b e)"),
                                S0[:, 0:T].rearrange("p (j n) -> p j n", j=J)[:, :, 0:BG * E]).then_inc(posT_ready, 1)
                dve.wait_ge(posT_ready, g + 1)
                for b in range(BG):
                    n = g * BG + b
                    if b >= 2:
                        dve.wait_ge(xin_psum, DC * (n - 1))
                        dve.wait_ge(gs_ready, n - 1)
                    for j in range(J):
                        ins = dve.tensor_tensor(Sel[:, b % 2, j], iota1[:, :].unsqueeze(1).broadcast_to([P, E, CAP]),
                                                posT[:, j, b, :].unsqueeze(2).broadcast_to([P, E, CAP]), ALU.is_equal)
                    ins.then_inc(sel_ready, 1)

            dve.memset(ones_f[:, :], 1.0).then_inc(consts_ready, 1)
            dve.memset(ones_b[:, :], 1.0).then_inc(consts_ready, 1)
            dve.memset(posm[:, :], 0.0).then_inc(consts_ready, 1)
            dve.wait_ge(setup_b, 5 * 16)
            for half, row in enumerate((con, co)):
                src = row[0:1, 0:D].rearrange("o (t d two) -> o two t d", d=DK, two=2)
                hk = H // 2
                dve.tensor_copy(bias_row[0:1, D // 2 * half:D // 2 * (half + 1)].rearrange("o (t d) -> o t d", d=DK), src[:, 0])
                dve.tensor_copy(bias_row[0:1, D:2 * D].rearrange("o (d t) -> o t d", t=H)[:, hk * half:hk * (half + 1), :], src[:, 1]).then_inc(bias_rows, 1)
            dve.wait_ge(bias_rows, 2)
            for k in range(3):
                dve.tensor_copy(bias_pc[0:1, k, :], bias_row[0:1, :]).then_inc(bias_step, 1)
                dve.wait_ge(bias_step, 2 * k + 1)
                if k < 2:
                    dve.tensor_tensor(bias_row[0:1, :], bias_row[0:1, :], bias_pc[0:1, k, :], ALU.subtract).then_inc(bias_step, 1)
                    dve.wait_ge(bias_step, 2 * k + 2)
            for c in range(DC):
                dve.wait_ge(setup_t, 2 * c + 1)
                src = bank[4 + 2 * c]
                dve.tensor_copy(wkvT[:, c, 0:D], src[:, 0:D])
                dve.tensor_copy(wkvT[:, c, D:2 * D].rearrange("p (d t) -> p t d", t=H),
                                src[:, D:2 * D].rearrange("p (t d) -> p t d", d=DK)).then_inc(setup_ev, 1)
                dve.wait_ge(setup_t, 2 * c + 2)
                src = bank[5 + 2 * c]
                dve.tensor_copy(woT[:, c, :], src[:, 0:D])
                dve.tensor_copy(gwT[:, c, :], src[:, D:D + E]).then_inc(setup_ev, 1)
            dve.memset(mv[:, 1, :], 1.0).then_inc(mv_set, 1)
            dve.wait_ge(mv_set, 1)
            dve.wait_ge(gates_tanh, 1)

            begin_attention(0)
            for i in range(TG):
                tile_of(0, i)
            end_attention(0)
            gate_softmax(0)
            choose_tokens(0)
            with dve.Fori(0, G - 1) as g:
                selection(g)
                begin_attention(g + 1)
                for i in range(TG):
                    tile_of(g + 1, i)
                end_attention(g + 1)
                gate_softmax(g + 1)
                choose_tokens(g + 1)
                last_sums(g)
            selection(G - 1)
            last_sums(G - 1)

        @block.scalar
        def _(act):
            def copy(dst, src, done):
                act.activation(dst, src, ACT.Copy).then_inc(done, 1)

            def take_ctT(g, i):
                act.wait_ge(ctT_psum, g * TG + i + 1)
                copy(ctT[:, :, :].rearrange("p c t -> p (c t)"), S0[:, 0:D], ctT_ready)

            def take_kv(g, i):
                t = g * TG + i
                act.wait_ge(kv_psum, t + 1)
                if not (isinstance(g, int) and g == 0 and i < 2):
                    act.wait_ge(cop_done, t - 1)
                copy(kvs[:, i % 2, :], KV[i % 2][:, :], kvs_ready)

            def exponentials(g, i):
                t = g * TG + i
                act.wait_ge(Sc_ready, t + 1)
                if not (isinstance(g, int) and g == 0 and i == 0):
                    act.wait_ge(cov_done, t)
                    act.wait_ge(cop_done, t)
                act.activation(Ex[:, :], Sc[:, :], ACT.Exp, scale=DK ** -0.5).then_inc(E_ready, 1)

            def take_coT(g, i):
                act.wait_ge(coT_psum, g * TG + i + 1)
                copy(coT[:, :, :].rearrange("p c t -> p (c t)"), S1[:, 0:D], coT_ready)

            def take_xnT(g, i):
                act.wait_ge(xnT_psum, g * TG + i + 1)
                copy(xnT[:, :, :].rearrange("p c t -> p (c t)"), S1[:, 0:D], xnT_ready)

            def take_logits(g, i):
                act.wait_ge(lg_psum, g * TG + i + 1)
                copy(lg[:, i % J, i // J, :], S0[:, 0:E], lg_ready)

            def gelu(g, e, k):
                act.wait_ge(h_psum, 4 * (g * E + e) + k + 1)
                act.activation(hT[:, 2 * k:2 * k + 2, :].rearrange("p f n -> p (f n)"), HB[k % 2][:, :], ACT.Gelu).then_inc(h_ready, 1)

            def take_y(g, e, pair):
                n = g * E + e
                act.wait_ge(y_psum, 2 * n + pair + 1)
                if e >= 2:
                    for beta in range(2):
                        act.wait_ge(y_moved[e % 2][beta], 16 * (g * (E // 2) + e // 2))
                copy(ys[:, e % 2, pair, :], YB[pair][:, 0:D], y_ready)

            def begin_experts(g):
                for b in range(BG):
                    n = g * BG + b
                    for j in range(J):
                        act.wait_ge(gt_psum, J * n + j + 1)
                        copy(GT[:, b, :, P * j:P * (j + 1)], YB[j][:, :].rearrange("p (e t) -> p e t", e=EP), gt_ready)
                    for c in range(DC):
                        act.wait_ge(xin_psum, DC * n + c + 1)
                        copy(xin[:, c, :, b, :], HB[c][:, :].rearrange("p (e s) -> p e s", e=E), xin_ready)

            def gate_exp(g):
                act.wait_ge(gstep, 3 * g + 2)
                act.activation(pe_[:, :, :, :].rearrange("p j b e -> p (j b e)"),
                               lgs[:, :, :, :].rearrange("p j b e -> p (j b e)"), ACT.Exp).then_inc(gexp_ready, 1)

            def slots(ga, gf):
                for s in range(TG):
                    if ga is not None and s + 1 < TG:
                        take_ctT(ga, s + 1)
                    if ga is not None and s > 0:
                        take_coT(ga, s - 1)
                    if gf is not None:
                        gelu(gf, s, 0)
                        gelu(gf, s, 1)
                    if ga is not None and s + 1 < TG:
                        take_kv(ga, s + 1)
                    if ga is not None:
                        exponentials(ga, s)
                    if gf is not None:
                        gelu(gf, s, 2)
                        gelu(gf, s, 3)
                    if ga is not None and s > 0:
                        take_xnT(ga, s - 1)
                    if gf is not None:
                        take_y(gf, s, 0)
                    if ga is not None and s > 0:
                        take_logits(ga, s - 1)
                    if gf is not None:
                        take_y(gf, s, 1)
                if ga is not None:
                    take_coT(ga, TG - 1)
                    take_xnT(ga, TG - 1)
                    take_logits(ga, TG - 1)
                    gate_exp(ga)

            act.wait_ge(setup_b, 5 * 16)
            act.activation(tanh_g[:, :], gates[:, :], ACT.Tanh).then_inc(gates_tanh, 1)
            take_ctT(0, 0)
            take_kv(0, 0)
            slots(0, None)
            with act.Fori(0, G - 1) as g:
                take_ctT(g + 1, 0)
                take_kv(g + 1, 0)
                begin_experts(g)
                slots(g + 1, g)
            begin_experts(G - 1)
            slots(None, G - 1)

        @block.tensor
        def _(pe):
            def transposes(dst, src, n):
                for c in range(n):
                    ins = pe.transpose(dst[:, P * c:P * (c + 1)], src[:, P * c:P * (c + 1)], ident[:, :])
                return ins

            def ctx_transposes(g, i):
                t = g * TG + i
                pe.wait_ge(c_loaded[i % 2], 16 * (g * (TG // 2) + i // 2) + 16)
                if i == 0:
                    if not isinstance(g, int):
                        pe.wait_ge(posT_ready, g)
                elif i >= 3:
                    pe.wait_ge(lg_ready, t - 2)
                transposes(S0, ct[:, i % 2, :], DC).then_inc(ctT_psum, 1)

            def project_kv(g, i):
                t = g * TG + i
                pe.wait_ge(ctT_ready, t + 1)
                if not (isinstance(g, int) and g == 0 and i < 2):
                    pe.wait_ge(cov_done, t - 1)
                for c in range(DC):
                    pe.matmul(KV[i % 2][:, :], ctT[:, c, :], wkvT[:, c, :], start=(c == 0), stop=False)
                pe.matmul(KV[i % 2][:, :], ones_b[:, :], bias_b[:, 0:2 * D], start=False, stop=True).then_inc(kv_psum, 1)

            def co_transposes(g, i):
                t = g * TG + i
                pe.wait_ge(con_ready, t + 1)
                if i == 0 and not isinstance(g, int):
                    pe.wait_ge(work_ready, g)
                transposes(S1, con[:, :], DC).then_inc(coT_psum, 1)

            def project_out(g, i):
                pe.wait_ge(coT_ready, g * TG + i + 1)
                for c in range(DC):
                    pe.matmul(S0[:, 0:D], coT[:, c, :], woT[:, c, :], start=(c == 0), stop=False)
                pe.matmul(S0[:, 0:D], ones_b[:, :], bias_b[:, 2 * D:3 * D], start=False, stop=True).then_inc(wo_psum, 1)

            def xn_transposes(g, i):
                pe.wait_ge(xn_ready, g * TG + i + 1)
                transposes(S1, xn[:, i, :], DC).then_inc(xnT_psum, 1)

            def logits(g, i):
                pe.wait_ge(xnT_ready, g * TG + i + 1)
                for c in range(DC):
                    ins = pe.matmul(S0[:, 0:E], xnT[:, c, :], gwT[:, c, :], start=(c == 0), stop=(c == DC - 1))
                ins.then_inc(lg_psum, 1)

            def hidden(g, e, k):
                n = g * E + e
                if k == 0:
                    pe.wait_ge(w1_loaded[e % 2], 16 * (g * (E // 2) + e // 2) + 16)
                if e == 0 and k < 2:
                    pe.wait_ge(xin_ready, DC * BG * (g + 1))
                else:
                    pe.wait_ge(h_ready, 4 * n + k - 1)
                for f in (2 * k, 2 * k + 1):
                    for c in range(DC):
                        ins = pe.matmul(HB[k % 2][:, D * (f % 2):D * (f % 2 + 1)], w1s[:, e % 2, c, P * f:P * (f + 1)],
                                        xin[:, c, e, :, :].rearrange("p b s -> p (b s)"), start=(c == 0), stop=(c == DC - 1))
                ins.then_inc(h_psum, 1)

            def outputs(g, e, pair):
                n = g * E + e
                if pair == 0:
                    pe.wait_ge(w2_loaded[e % 2], 16 * (g * (E // 2) + e // 2) + 16)
                    pe.wait_ge(h_ready, 4 * n + 4)
                if e == 0:
                    pe.wait_ge(gt_ready, J * BG * (g + 1))
                else:
                    pe.wait_ge(y_ready, 2 * (n - 1) + pair + 1)
                for f in range(FC):
                    ins = pe.matmul(YB[pair][:, 0:D], hT[:, f, P * pair:P * (pair + 1)], w2s[:, e % 2, f, :],
                                    start=(f == 0), stop=(f == FC - 1))
                ins.then_inc(y_psum, 1)

            def begin_experts(g):
                for b in range(BG):
                    n = g * BG + b
                    pe.wait_ge(gs_ready, n + 1)
                    for j in range(J):
                        if b > 0:
                            pe.wait_ge(gt_ready, J * (n - 1) + j + 1)
                        transposes(YB[j], Gs[:, j, :, :].rearrange("p e s -> p (e s)"), EP).then_inc(gt_psum, 1)
                    pe.wait_ge(sel_ready, n + 1)
                    for c in range(DC):
                        if b > 0:
                            pe.wait_ge(xin_ready, DC * (n - 1) + c + 1)
                        for j in range(J):
                            ins = pe.matmul(HB[c][:, :], xn[:, J * b + j, P * c:P * (c + 1)],
                                            Sel[:, b % 2, j, :, :].rearrange("p e s -> p (e s)"), start=(j == 0), stop=(j == J - 1))
                        ins.then_inc(xin_psum, 1)

            def end_experts(g):
                for i in range(TG):
                    b, j = i // J, i % J
                    if i == 0:
                        for moved in y_moved[0] + y_moved[1]:
                            pe.wait_ge(moved, 16 * (E // 2) * (g + 1))
                        pe.wait_ge(y_ready, 2 * E * (g + 1))
                    if i >= 4:
                        pe.wait_ge(fin_ready, TG * g + i - 3)
                    for ep in range(EP):
                        ins = pe.matmul(CB[i % 4][:, 0:D], GT[:, b, ep, P * j:P * (j + 1)], Y[:, b, ep, :],
                                        start=(ep == 0), stop=(ep == EP - 1))
                    ins.then_inc(comb_psum, 1)
                pe.wait_ge(fin_ready, TG * (g + 1))

            def slots(ga, gf):
                for s in range(TG):
                    if ga is not None and s + 1 < TG:
                        ctx_transposes(ga, s + 1)
                    if ga is not None and s > 0:
                        co_transposes(ga, s - 1)
                    if gf is not None:
                        hidden(gf, s, 0)
                        hidden(gf, s, 1)
                    if ga is not None and s + 1 < TG:
                        project_kv(ga, s + 1)
                    if ga is not None and s > 0:
                        project_out(ga, s - 1)
                    if gf is not None:
                        hidden(gf, s, 2)
                        hidden(gf, s, 3)
                    if ga is not None and s > 0:
                        xn_transposes(ga, s - 1)
                    if gf is not None:
                        outputs(gf, s, 0)
                    if ga is not None and s > 0:
                        logits(ga, s - 1)
                    if gf is not None:
                        outputs(gf, s, 1)

            def end_attention(g):
                co_transposes(g, TG - 1)
                project_out(g, TG - 1)
                xn_transposes(g, TG - 1)
                logits(g, TG - 1)
                pe.wait_ge(pr_ready, g + 1)
                for j in range(J):
                    ins = pe.transpose(S1[0:BG * E, P * j:P * (j + 1)], pr[:, j, :, :].rearrange("p b e -> p (b e)"), ident[:, :])
                ins.then_inc(prT_psum, 1)

            def position_transposes(g):
                pe.wait_ge(posm_ready, g + 1)
                for j in range(J):
                    ins = pe.transpose(S0[:, P * j:P * (j + 1)], posm[:, P * j:P * (j + 1)], ident[:, :])
                ins.then_inc(posT_psum, 1)

            pe.wait_ge(ident_ready, 2)
            pe.wait_ge(setup_loaded, 7 * 16)
            for c in range(DC):
                cols = slice(P * c, P * (c + 1))
                for a in range(4):
                    ins = pe.transpose(bank[4 + 2 * c][:, P * a:P * (a + 1)], wrow[:, a, cols], ident[:, :])
                ins.then_inc(setup_t, 1)
                for a in range(2):
                    pe.transpose(bank[5 + 2 * c][:, P * a:P * (a + 1)], wrow[:, 4 + a, cols], ident[:, :])
                pe.transpose(bank[5 + 2 * c][:, D:D + E], gwrow[:, cols], ident[0:E, 0:E]).then_inc(setup_t, 1)
            ctx_transposes(0, 0)
            pe.wait_ge(setup_ev, 4)
            pe.wait_ge(bias_moved, 3 * 16)
            project_kv(0, 0)
            slots(0, None)
            end_attention(0)
            position_transposes(0)
            with pe.Fori(0, G - 1) as g:
                ctx_transposes(g + 1, 0)
                project_kv(g + 1, 0)
                begin_experts(g)
                slots(g + 1, g)
                end_attention(g + 1)
                end_experts(g)
                position_transposes(g + 1)
            begin_experts(G - 1)
            slots(None, G - 1)
            end_experts(G - 1)


_INS = ['x', 'ctx_1024', 'g_xattn', 'g_ffn', 'L0_xattn_W_kv', 'L0_xattn_b_kv', 'L0_xattn_W_out', 'L0_xattn_b_out',
        'L0_ffn_gate_w', 'L0_ffn_w1', 'L0_ffn_w2']
_OUTS = [((16, 256, 256), 'float32')]


def kernel(**inputs):
    import numpy as _np
    import concourse.bacc as _bacc
    from concourse import mybir as _mybir
    from concourse.bass_utils import run_bass_kernel_spmd as _run

    nc = _bacc.Bacc("TRN2", target_bir_lowering=False, num_devices=1)
    arrays, args = {}, []
    for name in _INS:
        a = _np.ascontiguousarray(inputs[name])
        arrays[f"in_{name}_dram"] = a
        args.append(nc.dram_tensor(f"in_{name}_dram", a.shape, _mybir.dt.from_np(a.dtype), kind="ExternalInput").ap())
    for i, (shape, dtype) in enumerate(_OUTS):
        dt = _mybir.dt.from_np(_np.dtype(dtype))
        args.append(nc.dram_tensor(f"out_{i}_dram", shape, dt, kind="ExternalOutput").ap())
    flamingo_gated_block_kernel(nc, *args)
    r = _run(nc, [arrays], core_ids=[0])
    got = tuple(r.results[0][f"out_{i}_dram"] for i in range(len(_OUTS)))
    return got[0]
```

```python
from contextlib import ExitStack

import concourse.bass as bass
from concourse import mybir


def flamingo_gated_block_kernel(nc, x, ctx_in, g_xattn, g_ffn, W_kv, b_kv, W_out, b_out, gate_w, w1, w2, out):
    fp32 = mybir.dt.float32
    bf16 = mybir.dt.bfloat16
    f32r = mybir.dt.float32r
    ALU = mybir.AluOpType
    ACT = mybir.ActivationFunctionType
    AX = mybir.AxisListType

    B, T, D = x.shape
    E, _, F = w1.shape
    P = 128
    H = 16
    DK = D // H
    CAP = 2 * T // E
    G = 4
    BG = B // G
    J = T // P
    TG = BG * J
    DC = D // P
    FC = F // P
    EP = E // 2
    HV = 11
    HP = H - HV
    NR = TG + 2
    EPS = 1e-5
    assert 2 * CAP == P and TG == E and BG == 4

    x_t = x.rearrange("b (j p) c -> (b j) p c", p=P)
    c_t = ctx_in.rearrange("b (j p) c -> (b j) p c", p=P)
    o_t = out.rearrange("b (j p) c -> (b j) p c", p=P)
    x2_d = nc.dram_tensor("x2_scratch", [B * J, P, D], fp32).ap()
    w1_d = w1.rearrange("e (c p) f -> e p c f", p=P)
    w2_d = w2.rearrange("e (f p) d -> e p f d", p=P)

    es = ExitStack()
    with es:
        def sb(name, shape, dt=fp32):
            return es.enter_context(nc.sbuf_tensor(name, shape, dt))

        def sem(name):
            return es.enter_context(nc.semaphore(name))

        def sems(name, k):
            return [sem(f"{name}{i}") for i in range(k)]

        ident = sb("ident", [P, P])
        iota1 = sb("iota1", [P, CAP])
        ones_f = sb("ones_f", [P, T])
        ones_b = sb("ones_b", [3, P], bf16)
        neg_half = sb("neg_half", [P, 2])
        tanh_g = sb("tanh_g", [P, 2])
        gates = sb("gates", [P, 2])
        wkvT = sb("wkvT", [P, DC, 2 * D])
        woT = sb("woT", [P, DC, D])
        gwT = sb("gwT", [P, DC, E])
        bias_b = sb("bias_b", [3, 3 * D], bf16)

        xt = sb("xt", [P, 4, D])
        ct = sb("ct", [P, 2, D])
        ctT = sb("ctT", [P, DC, P])
        q = sb("q", [P, 2, D])
        kvs = sb("kvs", [P, 2, 2 * D])
        prod_v = sb("prod_v", [P, HV * DK * DK])
        prod_p = sb("prod_p", [P, HP * DK * DK])
        wrow = prod_v[:, 0:6 * D].rearrange("p (a c) -> p a c", c=D)
        bias_row = prod_v[0:1, 6 * D:9 * D]
        gwrow = prod_v[0:E, 9 * D:10 * D]
        bias_pc = prod_p[0:1, :].bitcast(bf16)[:, 0:9 * D].rearrange("o (k n) -> o k n", k=3)
        tree_a = sb("tree_a", [P, HP * DK * 8])
        tree_b = sb("tree_b", [P, HP * DK * 4])
        tree_c = sb("tree_c", [P, HP * DK * 2])
        S = sb("S", [P, H * DK])
        Sc = sb("Sc", [P, H * DK])
        mx = sb("mx", [P, H])
        Ex = sb("Ex", [P, H * DK])
        den = sb("den", [P, H])
        rden = sb("rden", [P, H])
        co = sb("co", [P, D])
        con = sb("con", [P, D])
        coT = sb("coT", [P, DC, P])
        x2 = sb("x2", [P, 2, D])
        st1 = sb("st1", [P, 6])
        st2 = sb("st2", [P, 6])
        mv = sb("mv", [P, 2, 2])
        ve = sb("ve", [P, 2])
        rs = sb("rs", [P, 2])
        xn = sb("xn", [P, 2, D])
        xnh = sb("xnh", [P, TG, D], f32r)
        xnl = sb("xnl", [P, TG, D], f32r)
        xnT = sb("xnT", [P, DC, P])

        lg = sb("lg", [P, J, BG, E])
        lgs = sb("lgs", [P, J, BG, E])
        gmx = sb("gmx", [P, J * BG])
        pe_ = sb("pe_", [P, J, BG, E])
        gsum = sb("gsum", [P, J * BG])
        grec = sb("grec", [P, J * BG])
        pr = sb("pr", [P, J, BG, E])
        work, mask, cum = (prod_v[0:BG * E, T * k:T * (k + 1)] for k in range(3))
        top8 = sb("top8", [BG * E, 8])
        spare = sb("spare", [P, 1])
        posm = sb("posm", [P, T])
        posT = sb("posT", [P, J, BG, E])
        Sel = sb("Sel", [P, BG, J, E, CAP], f32r)
        Gs = sb("Gs", [P, 2, J, E, CAP])

        xin = sb("xin", [P, DC, E, BG, CAP])
        GT = sb("GT", [P, BG, EP, T])
        w1s = sb("w1s", [P, 2, DC, F])
        w2s = sb("w2s", [P, 2, FC, D])
        hT = sb("hT", [P, 2, FC, BG * CAP])
        ys = sb("ys", [P, 2, 2, D])
        Y = sb("Y", [P, BG, EP, D])
        xr = sb("xr", [P, 4, D])

        bank = [es.enter_context(nc.psum_tensor(f"bank{i}", [P, 512], fp32)) for i in range(8)]
        KV, S0, S1, HB, YB = bank[0:2], bank[2], bank[3], bank[4:6], bank[6:8]
        CB = HB + YB

        setup_loaded, setup_b, gates_tanh = sem("setup_loaded"), sem("setup_b"), sem("gates_tanh")
        ident_ready, consts_ready = sem("ident_ready"), sem("consts_ready")
        setup_t, setup_ev = sem("setup_t"), sem("setup_ev")
        bias_rows, bias_step, bias_moved = sem("bias_rows"), sem("bias_step"), sem("bias_moved")
        mv_set, grec_ready = sem("mv_set"), sem("grec_ready")
        x_loaded, c_loaded = sems("x_loaded", 4), sems("c_loaded", 2)
        ctT_psum, ctT_ready, kv_psum, kvs_ready = sem("ctT_psum"), sem("ctT_ready"), sem("kv_psum"), sem("kvs_ready")
        st_x, st_x2, mv_ready, ve_ready, rs_ready = sem("st_x"), sem("st_x2"), sem("mv_ready"), sem("ve_ready"), sem("rs_ready")
        q_ready, xn_ready = sem("q_ready"), sem("xn_ready")
        xnh_ready, xnl_ready = sem("xnh_ready"), sem("xnl_ready")
        prodv_s, prodp_s, tree_s = sem("prodv_s"), sem("prodp_s"), sem("tree_s")
        Sv_done, Sp_done, mx_done, Sc_ready, E_ready, den_done, rden_done = (
            sem("Sv_done"), sem("Sp_done"), sem("mx_done"), sem("Sc_ready"), sem("E_ready"), sem("den_done"), sem("rden_done"))
        cov_done, cop_done, con_ready = sem("cov_done"), sem("cop_done"), sem("con_ready")
        coT_psum, coT_ready, wo_psum, x2_ready, x2_stored = (
            sem("coT_psum"), sem("coT_ready"), sem("wo_psum"), sem("x2_ready"), sems("x2_stored", 2))
        xnT_psum, xnT_ready, lg_psum, lg_ready = sem("xnT_psum"), sem("xnT_ready"), sem("lg_psum"), sem("lg_ready")
        gstep, gexp_ready, pr_ready, prT_psum, work_ready, found8, removed8, mask_ready, cum_ready, posm_ready = (
            sem("gstep"), sem("gexp_ready"), sem("pr_ready"), sem("prT_psum"), sem("work_ready"), sem("found8"),
            sem("removed8"), sem("mask_ready"), sem("cum_ready"), sem("posm_ready"))
        posT_psum, posT_ready, sel_ready, gs_ready = sem("posT_psum"), sem("posT_ready"), sem("sel_ready"), sem("gs_ready")
        gt_psum, gt_ready, xin_psum, xin_ready = sem("gt_psum"), sem("gt_ready"), sem("xin_psum"), sem("xin_ready")
        w1_loaded, w2_loaded = sems("w1_loaded", 2), sems("w2_loaded", 2)
        h_psum, h_ready, y_psum, y_ready = sem("h_psum"), sem("h_ready"), sem("y_psum"), sem("y_ready")
        y_moved = [sems("y_moved_even", 2), sems("y_moved_odd", 2)]
        comb_psum, fin_ready = sem("comb_psum"), sem("fin_ready")
        xr_loaded, out_stored = sems("xr_loaded", 4), sems("out_stored", 4)
        out_done = sem("out_done")

        block = es.enter_context(nc.Block())

        @block.sync
        def _(sp):
            def load_x(g, i):
                t = g * TG + i
                if not (isinstance(g, int) and g == 0 and i < 4):
                    sp.wait_ge(x2_ready, t - 3)
                sp.dma_start(xt[:, i % 4, :], x_t[bass.ds(t, 1)].rearrange("o p c -> p (o c)")).then_inc(x_loaded[i % 4], 16)

            def load_c(g, i):
                t = g * TG + i
                if not (isinstance(g, int) and g == 0 and i < 2):
                    sp.wait_ge(ctT_psum, t - 1)
                sp.dma_start(ct[:, i % 2, :], c_t[bass.ds(t, 1)].rearrange("o p c -> p (o c)")).then_inc(c_loaded[i % 2], 16)

            def store_x2(g, i, known=False):
                t = g * TG + i
                if not known:
                    sp.wait_ge(x2_ready, t + 1)
                sp.dma_start(x2_d[bass.ds(t, 1)].rearrange("o p c -> p (o c)"), x2[:, i % 2, :]).then_inc(x2_stored[i % 2], 16)

            def load_w1(g, e):
                if not (isinstance(g, int) and g == 0 and e < 2):
                    sp.wait_ge(h_psum, 4 * (g * E + e - 1))
                sp.dma_start(w1s[:, e % 2, :, :], w1_d[e % E]).then_inc(w1_loaded[e % 2], 16)

            def load_w2(g, e):
                if not (isinstance(g, int) and g == 0 and e < 2):
                    sp.wait_ge(y_psum, 2 * (g * E + e - 1))
                sp.dma_start(w2s[:, e % 2, :, :], w2_d[e % E]).then_inc(w2_loaded[e % 2], 16)

            def move_y(g, e):
                n = g * E + e
                sp.wait_ge(y_ready, 2 * n + 2)
                for beta in range(2):
                    rows = slice(CAP * (e % 2), CAP * (e % 2) + CAP)
                    sp.dma_start(Y[rows, beta:BG:2, e // 2, :], ys[CAP * beta:CAP * beta + CAP, e % 2, :, :]).then_inc(y_moved[e % 2][beta], 16)

            def finish(g):
                for i in range(TG):
                    t = g * TG + i
                    u = i % 4
                    if i >= 4:
                        sp.wait_ge(out_stored[u], 16 * (g + 1))
                    if i == 0 and isinstance(g, int):
                        for stored in x2_stored:
                            sp.wait_ge(stored, 16 * (TG // 2) * (g + 1))
                    sp.dma_start(xr[:, u, :], x2_d[bass.ds(t, 1)].rearrange("o p c -> p (o c)")).then_inc(xr_loaded[u], 16)
                    if i >= 3:
                        store_out(g, i - 3)
                for i in range(TG - 3, TG):
                    store_out(g, i)
                sp.wait_ge(out_done, 16 * (TG - 4) * (g + 1))

            def store_out(g, i):
                t = g * TG + i
                sp.wait_ge(fin_ready, t + 1)
                sp.dma_start(o_t[bass.ds(t, 1)].rearrange("o p c -> p (o c)"), xr[:, i % 4, :]).then_inc(out_stored[i] if i < 4 else out_done, 16)

            sp.dma_start(ct[:, 0, :], c_t[0]).then_inc(c_loaded[0], 16)
            for a in range(DC):
                rows = W_kv[2 * P * a:2 * P * (a + 1), :].rearrange("(n two) c -> two n c", two=2)
                for kv in range(2):
                    sp.dma_start(wrow[:, 2 * kv + a, :], rows[kv]).then_inc(setup_loaded, 16)
                sp.dma_start(wrow[:, 4 + a, :], W_out[P * a:P * (a + 1), :]).then_inc(setup_loaded, 16)
            sp.dma_start(gwrow[:, :], gate_w).then_inc(setup_loaded, 16)
            sp.dma_start(gates[:, 0:1], g_xattn.rearrange("(a n) -> a n", a=1).broadcast_to([P, 1])).then_inc(setup_b, 16)
            sp.dma_start(gates[:, 1:2], g_ffn.rearrange("(a n) -> a n", a=1).broadcast_to([P, 1])).then_inc(setup_b, 16)
            sp.dma_start(con[0:1, 0:D], b_kv.rearrange("(o a n) -> o a n", o=1, a=2)[:, 0, :]).then_inc(setup_b, 16)
            sp.dma_start(co[0:1, 0:D], b_kv.rearrange("(o a n) -> o a n", o=1, a=2)[:, 1, :]).then_inc(setup_b, 16)
            sp.dma_start(bias_row[0:1, 2 * D:3 * D], b_out.rearrange("(o n) -> o n", o=1)).then_inc(setup_b, 16)
            sp.dma_start(xt[:, 0, :], x_t[0]).then_inc(x_loaded[0], 16)
            load_x(0, 1)
            load_c(0, 1)
            sp.wait_ge(bias_step, 5)
            for k in range(3):
                sp.dma_start(bias_b[k:k + 1, :], bias_pc[0:1, k, :]).then_inc(bias_moved, 16)
            load_x(0, 2)
            for e in range(2):
                load_w1(0, e)
                load_w2(0, e)

            def slot_loads(g, i):
                if i + 3 < TG:
                    load_x(g, i + 3)
                if i + 2 < TG:
                    load_c(g, i + 2)

            for i in range(TG):
                slot_loads(0, i)
                if i > 0:
                    store_x2(0, i - 1)
            store_x2(0, TG - 1)
            with sp.Fori(0, G - 1) as g:
                for s in range(TG):
                    slot_loads(g + 1, s)
                    if s > 0:
                        store_x2(g + 1, s - 1)
                    load_w1(g, s + 2)
                    if s > 0:
                        load_w2(g, s + 1)
                        move_y(g, s - 1)
                move_y(g, E - 1)
                load_w2(g, E + 1)
                finish(g)
                store_x2(g + 1, TG - 1, known=True)
            for s in range(E):
                if s + 2 < E:
                    load_w1(G - 1, s + 2)
                if s > 0:
                    if s + 1 < E:
                        load_w2(G - 1, s + 1)
                    move_y(G - 1, s - 1)
            move_y(G - 1, E - 1)
            finish(G - 1)
            for stored in x2_stored:
                sp.wait_ge(stored, 16 * B * J // 2)

        @block.gpsimd
        def _(pool):
            def share(in0, in1, dst, n_tree, done):
                pv = prod_p[:, :].rearrange("p (h a b) -> p h a b", a=DK, b=DK)
                pool.tensor_tensor(pv, in0, in1, ALU.mult).then_inc(prodp_s, 1)
                pool.wait_ge(prodp_s, n_tree + 1)
                src = prod_p[:, :].rearrange("p (r b) -> p r b", b=DK)
                for k, buf in enumerate((tree_a, tree_b, tree_c)):
                    w = DK >> (k + 1)
                    nxt = buf[:, :].rearrange("p (r b) -> p r b", b=w)
                    pool.tensor_tensor(nxt, src[:, :, 0:w], src[:, :, w:2 * w], ALU.add).then_inc(tree_s, 1)
                    pool.wait_ge(tree_s, 3 * n_tree + k + 1)
                    src = nxt
                pool.tensor_tensor(dst.rearrange("p (r b) -> p r b", b=1), src[:, :, 0:1], src[:, :, 1:2], ALU.add).then_inc(done, 1)

            def rsqrt(n):
                pool.wait_ge(ve_ready, n + 1)
                pool.tensor_tensor(rs[:, :], ve[:, :], neg_half[:, :], ALU.pow).then_inc(rs_ready, 1)

            def tile_of(g, i):
                t = g * TG + i
                qi = q[:, i % 2, :].rearrange("p (h d) -> p h d", d=DK)[:, HV:H, :]
                Kv = kvs[:, i % 2, 0:D].rearrange("p (t d) -> p t d", d=DK)
                Vv = kvs[:, i % 2, D:2 * D].rearrange("p (d t) -> p d t", t=DK)
                Ev = Ex[:, :].rearrange("p (h t) -> p h t", t=DK)[:, HV:H, :]
                full = [P, HP, DK, DK]
                pool.wait_ge(q_ready, t + 1)
                pool.wait_ge(kvs_ready, t + 1)
                if not (isinstance(g, int) and g == 0 and i == 0):
                    pool.wait_ge(Sc_ready, t)
                share(Kv.unsqueeze(1).broadcast_to(full), qi.unsqueeze(2).broadcast_to(full),
                      S[:, HV * DK:H * DK], 2 * t, Sp_done)
                rsqrt(NR * g + i + 1)
                pool.wait_ge(E_ready, t + 1)
                if not (isinstance(g, int) and g == 0 and i == 0):
                    pool.wait_ge(con_ready, t)
                share(Vv.unsqueeze(1).broadcast_to(full), Ev.unsqueeze(2).broadcast_to(full),
                      co[:, HV * DK:H * DK], 2 * t + 1, cop_done)

            def attention(g):
                for i in range(TG):
                    tile_of(g, i)
                rsqrt(NR * g + TG + 1)

            def gated_selection(g):
                for b in range(BG):
                    n = g * BG + b
                    pool.wait_ge(sel_ready, n + 1)
                    if b >= 2:
                        pool.wait_ge(gt_psum, J * (n - 1))
                    for j in range(J):
                        ins = pool.tensor_tensor(Gs[:, b % 2, j], Sel[:, b, j].bitcast(fp32), pr[:, j, b, :].unsqueeze(2).broadcast_to([P, E, CAP]), ALU.mult)
                    ins.then_inc(gs_ready, 1)

            pool.iota(iota1[:, :], pattern=[[1, CAP]], base=1, channel_multiplier=0,
                      allow_small_or_imprecise_dtypes=True).then_inc(consts_ready, 1)
            pool.memset(neg_half[:, :], -0.5).then_inc(consts_ready, 1)
            pool.memset(ident[:, :], 0.0).then_inc(ident_ready, 1)
            pool.wait_ge(ident_ready, 1)
            pool.affine_select(out=ident[:, :], in_=ident[:, :], compare_op=ALU.not_equal, fill=1.0,
                               base=0, pattern=[[-1, P]], channel_multiplier=1).then_inc(ident_ready, 1)
            pool.wait_ge(consts_ready, 2)
            rsqrt(0)
            attention(0)
            with pool.Fori(0, G - 1) as g:
                rsqrt(NR * (g + 1))
                gated_selection(g)
                attention(g + 1)
            gated_selection(G - 1)

        @block.vector
        def _(dve):
            def first(g, i=0):
                return isinstance(g, int) and g == 0 and i == 0

            def wait_apart(sem, value):
                dve.wait_ge(sem, value)
                dve.memset(spare[:, :], 0.0)

            def products(in0, in1, dst, n, done):
                pv = prod_v[:, :].rearrange("p (h a b) -> p h a b", a=DK, b=DK)
                dve.tensor_tensor(pv, in0, in1, ALU.mult).then_inc(prodv_s, 1)
                dve.wait_ge(prodv_s, n + 1)
                dve.tensor_reduce(dst, prod_v[:, :].rearrange("p (r b) -> p r b", b=DK), axis=AX.X, op=ALU.add).then_inc(done, 1)

            def stats(g, i_x, i_x2):
                if i_x is not None:
                    t = g * TG + i_x
                    dve.wait_ge(x_loaded[i_x % 4], 16 * (g * (TG // 4) + i_x // 4) + 16)
                    dve.bn_stats(st1[:, :], xt[:, i_x % 4, :]).then_inc(st_x, 1)
                    wait_apart(st_x, t + 1)
                    dve.bn_aggr(mv[:, 0, :], st1[:, :]).then_inc(mv_ready, 1)
                if i_x2 is not None:
                    t = g * TG + i_x2
                    dve.wait_ge(x2_ready, t + 1)
                    dve.bn_stats(st2[:, :], x2[:, i_x2 % 2, :]).then_inc(st_x2, 1)
                    wait_apart(st_x2, t + 1)
                    dve.bn_aggr(mv[:, 1, :], st2[:, :]).then_inc(mv_ready, 1)
                done = (TG if i_x is None else i_x + 1) + (0 if i_x2 is None else i_x2 + 1)
                dve.wait_ge(mv_ready, 2 * TG * g + done)
                dve.tensor_scalar(ve[:, :], mv[:, :, 1], EPS, None, ALU.add).then_inc(ve_ready, 1)

            def make_q(g, i):
                dve.tensor_scalar(q[:, i % 2, :], xt[:, i % 4, :], mv[:, 0, 0:1], rs[:, 0:1], ALU.subtract, ALU.mult).then_inc(q_ready, 1)

            def make_xn(g, i):
                if i == 0:
                    dve.wait_ge(xin_psum, DC * BG * g)
                dve.tensor_scalar(xn[:, i % 2, :], x2[:, i % 2, :], mv[:, 1, 0:1], rs[:, 1:2], ALU.subtract, ALU.mult).then_inc(xn_ready, 1)

            def split_xn(g, i):
                dve.wait_ge(xnh_ready, g * TG + i + 1)
                dve.tensor_tensor(xnl[:, i, :], xn[:, i % 2, :], xnh[:, i, :].bitcast(fp32), ALU.subtract).then_inc(xnl_ready, 1)

            def residual(g, i):
                t = g * TG + i
                dve.wait_ge(wo_psum, t + 1)
                if not (isinstance(g, int) and g == 0 and i < 2):
                    dve.wait_ge(x2_stored[i % 2], 16 * (g * (TG // 2) + i // 2))
                dve.scalar_tensor_tensor(x2[:, i % 2, :], S0[:, 0:D], tanh_g[:, 0:1], xt[:, i % 4, :],
                                         ALU.mult, ALU.add).then_inc(x2_ready, 1)

            def tile_of(g, i):
                t = g * TG + i
                full = [P, HV, DK, DK]
                kvp = KV[i % 2]
                Kp = kvp[:, 0:D].rearrange("p (t d) -> p t d", d=DK)
                Vp = kvp[:, D:2 * D].rearrange("p (d t) -> p d t", t=DK)
                qi = q[:, i % 2, :].rearrange("p (h d) -> p h d", d=DK)[:, 0:HV, :]
                Ev = Ex[:, :].rearrange("p (h t) -> p h t", t=DK)
                dve.wait_ge(kvs_ready, t + 1)
                dve.wait_ge(q_ready, t + 1)
                products(Kp.unsqueeze(1).broadcast_to(full), qi.unsqueeze(2).broadcast_to(full), S[:, 0:HV * DK], 2 * t, Sv_done)
                if i > 0:
                    residual(g, i - 1)
                stats(g, i + 1 if i + 1 < TG else None, i - 1 if i > 0 else None)
                dve.wait_ge(Sp_done, t + 1)
                dve.wait_ge(Sv_done, t + 1)
                Sv = S[:, :].rearrange("p (h t) -> p h t", t=DK)
                dve.reduce_max(mx[:, :], Sv, AX.X).then_inc(mx_done, 1)
                dve.wait_ge(mx_done, t + 1)
                if not first(g, i):
                    dve.wait_ge(E_ready, t)
                dve.tensor_tensor(Sc[:, :].rearrange("p (h t) -> p h t", t=DK), Sv,
                                  mx[:, :].unsqueeze(2).broadcast_to([P, H, DK]), ALU.subtract).then_inc(Sc_ready, 1)
                dve.wait_ge(rs_ready, NR * g + i + 2)
                if i + 1 < TG:
                    if not (isinstance(g, int) and g == 0 and i == 0):
                        dve.wait_ge(cop_done, t)
                    make_q(g, i + 1)
                if i > 0:
                    make_xn(g, i - 1)
                dve.wait_ge(E_ready, t + 1)
                dve.tensor_reduce(den[:, :], Ev, axis=AX.X, op=ALU.add).then_inc(den_done, 1)
                products(Vp.unsqueeze(1).broadcast_to(full), Ev[:, 0:HV, :].unsqueeze(2).broadcast_to(full), co[:, 0:HV * DK], 2 * t + 1, cov_done)
                if i > 0:
                    split_xn(g, i - 1)
                dve.wait_ge(den_done, t + 1)
                dve.reciprocal(rden[:, :], den[:, :]).then_inc(rden_done, 1)
                dve.wait_ge(rden_done, t + 1)
                dve.wait_ge(cop_done, t + 1)
                dve.wait_ge(cov_done, t + 1)
                if not first(g, i):
                    dve.wait_ge(coT_psum, t)
                dve.tensor_tensor(con[:, :].rearrange("p (h d) -> p h d", d=DK), co[:, :].rearrange("p (h d) -> p h d", d=DK),
                                  rden[:, :].unsqueeze(2).broadcast_to([P, H, DK]), ALU.mult).then_inc(con_ready, 1)

            def first_q(g):
                dve.wait_ge(rs_ready, NR * g + 1)
                make_q(g, 0)

            def end_attention(g):
                residual(g, TG - 1)
                stats(g, None, TG - 1)
                dve.wait_ge(rs_ready, NR * g + NR)
                make_xn(g, TG - 1)
                split_xn(g, TG - 1)

            def gate_softmax(g):
                v8 = lambda m: m[:, :, :, :].rearrange("p j b e -> p (j b) e")
                bc = lambda m: m[:, :].unsqueeze(2).broadcast_to([P, J * BG, E])
                dve.wait_ge(lg_ready, TG * g + TG)
                dve.reduce_max(gmx[:, :], v8(lg), AX.X).then_inc(gstep, 1)
                dve.wait_ge(gstep, 3 * g + 1)
                dve.tensor_tensor(v8(lgs), v8(lg), bc(gmx), ALU.subtract).then_inc(gstep, 1)
                dve.wait_ge(gexp_ready, g + 1)
                dve.reduce_sum(gsum[:, :], v8(pe_), AX.X).then_inc(gstep, 1)
                dve.wait_ge(gstep, 3 * g + 3)
                dve.reciprocal(grec[:, :], gsum[:, :]).then_inc(grec_ready, 1)
                dve.wait_ge(grec_ready, g + 1)
                dve.tensor_tensor(v8(pr), v8(pe_), bc(grec), ALU.mult).then_inc(pr_ready, 1)

            def choose_tokens(g, gl):
                dve.wait_ge(prT_psum, g + 1)
                dve.tensor_copy(work[:, :], S1[0:BG * E, 0:T]).then_inc(work_ready, 1)
                wait_apart(work_ready, g + 1)
                for r in range(CAP // 8):
                    n = g * (CAP // 8) + r
                    dve.max(top8[:, :], work[:, :]).then_inc(found8, 1)
                    wait_apart(found8, n + 1)
                    dve.match_replace(work[:, :], top8[:, :], work[:, :], -1.0).then_inc(removed8, 1)
                    if gl is not None and r < TG - 1:
                        last_sum(gl, r)
                    wait_apart(removed8, n + 1)
                dve.tensor_scalar(mask[:, :], work[:, :], 0.0, None, ALU.is_lt).then_inc(mask_ready, 1)
                dve.wait_ge(mask_ready, g + 1)
                dve.tensor_tensor_scan(cum[:, :], ones_f[0:BG * E, :], mask[:, :], 0.0, ALU.mult, ALU.add).then_inc(cum_ready, 1)
                dve.wait_ge(cum_ready, g + 1)
                dve.tensor_tensor(posm[0:BG * E, :], cum[:, :], mask[:, :], ALU.mult).then_inc(posm_ready, 1)
                if gl is not None:
                    last_sum(gl, TG - 1)

            def last_sum(g, i):
                dve.wait_ge(comb_psum, g * TG + i + 1)
                dve.wait_ge(xr_loaded[i % 4], 16 * (g * (TG // 4) + i // 4) + 16)
                dve.scalar_tensor_tensor(xr[:, i % 4, :], CB[i % 4][:, 0:D], tanh_g[:, 1:2], xr[:, i % 4, :],
                                         ALU.mult, ALU.add).then_inc(fin_ready, 1)

            def selection(g):
                dve.wait_ge(posT_psum, g + 1)
                dve.tensor_copy(posT[:, :, :, :].rearrange("p j b e -> p j (b e)"),
                                S0[:, 0:T].rearrange("p (j n) -> p j n", j=J)[:, :, 0:BG * E]).then_inc(posT_ready, 1)
                dve.wait_ge(posT_ready, g + 1)
                for b in range(BG):
                    for j in range(J):
                        ins = dve.tensor_tensor(Sel[:, b, j], iota1[:, :].unsqueeze(1).broadcast_to([P, E, CAP]),
                                                posT[:, j, b, :].unsqueeze(2).broadcast_to([P, E, CAP]), ALU.is_equal)
                    ins.then_inc(sel_ready, 1)

            dve.memset(ones_f[:, :], 1.0).then_inc(consts_ready, 1)
            dve.memset(ones_b[:, :], 1.0).then_inc(consts_ready, 1)
            dve.memset(posm[:, :], 0.0).then_inc(consts_ready, 1)
            dve.wait_ge(setup_b, 5 * 16)
            for half, row in enumerate((con, co)):
                src = row[0:1, 0:D].rearrange("o (t d two) -> o two t d", d=DK, two=2)
                hk = H // 2
                dve.tensor_copy(bias_row[0:1, D // 2 * half:D // 2 * (half + 1)].rearrange("o (t d) -> o t d", d=DK), src[:, 0])
                dve.tensor_copy(bias_row[0:1, D:2 * D].rearrange("o (d t) -> o t d", t=H)[:, hk * half:hk * (half + 1), :], src[:, 1]).then_inc(bias_rows, 1)
            dve.wait_ge(bias_rows, 2)
            for k in range(3):
                dve.tensor_copy(bias_pc[0:1, k, :], bias_row[0:1, :]).then_inc(bias_step, 1)
                dve.wait_ge(bias_step, 2 * k + 1)
                if k < 2:
                    dve.tensor_tensor(bias_row[0:1, :], bias_row[0:1, :], bias_pc[0:1, k, :], ALU.subtract).then_inc(bias_step, 1)
                    dve.wait_ge(bias_step, 2 * k + 2)
            for c in range(DC):
                dve.wait_ge(setup_t, 2 * c + 1)
                src = bank[4 + 2 * c]
                dve.tensor_copy(wkvT[:, c, 0:D], src[:, 0:D])
                dve.tensor_copy(wkvT[:, c, D:2 * D].rearrange("p (d t) -> p t d", t=H),
                                src[:, D:2 * D].rearrange("p (t d) -> p t d", d=DK)).then_inc(setup_ev, 1)
                dve.wait_ge(setup_t, 2 * c + 2)
                src = bank[5 + 2 * c]
                dve.tensor_copy(woT[:, c, :], src[:, 0:D])
                dve.tensor_copy(gwT[:, c, :], src[:, D:D + E]).then_inc(setup_ev, 1)
            dve.memset(mv[:, 1, :], 1.0).then_inc(mv_set, 1)
            dve.wait_ge(mv_set, 1)
            dve.wait_ge(gates_tanh, 1)

            stats(0, 0, None)
            first_q(0)
            for i in range(TG):
                tile_of(0, i)
            end_attention(0)
            gate_softmax(0)
            choose_tokens(0, None)
            with dve.Fori(0, G - 1) as g:
                stats(g + 1, 0, None)
                selection(g)
                first_q(g + 1)
                for i in range(TG):
                    tile_of(g + 1, i)
                end_attention(g + 1)
                gate_softmax(g + 1)
                choose_tokens(g + 1, g)
            selection(G - 1)
            for i in range(TG):
                last_sum(G - 1, i)

        @block.scalar
        def _(act):
            def copy(dst, src, done):
                act.activation(dst, src, ACT.Copy).then_inc(done, 1)

            def take_ctT(g, i):
                act.wait_ge(ctT_psum, g * TG + i + 1)
                copy(ctT[:, :, :].rearrange("p c t -> p (c t)"), S0[:, 0:D], ctT_ready)

            def take_kv(g, i):
                t = g * TG + i
                act.wait_ge(kv_psum, t + 1)
                if not (isinstance(g, int) and g == 0 and i < 2):
                    act.wait_ge(cop_done, t - 1)
                copy(kvs[:, i % 2, :], KV[i % 2][:, :], kvs_ready)

            def exponentials(g, i):
                t = g * TG + i
                act.wait_ge(Sc_ready, t + 1)
                if not (isinstance(g, int) and g == 0 and i == 0):
                    act.wait_ge(cov_done, t)
                    act.wait_ge(cop_done, t)
                act.activation(Ex[:, :], Sc[:, :], ACT.Exp, scale=DK ** -0.5).then_inc(E_ready, 1)

            def take_coT(g, i):
                act.wait_ge(coT_psum, g * TG + i + 1)
                copy(coT[:, :, :].rearrange("p c t -> p (c t)"), S1[:, 0:D], coT_ready)

            def round_xn(g, i):
                act.wait_ge(xn_ready, g * TG + i + 1)
                copy(xnh[:, i, :], xn[:, i % 2, :], xnh_ready)

            def take_xnT(g, i):
                act.wait_ge(xnT_psum, g * TG + i + 1)
                copy(xnT[:, :, :].rearrange("p c t -> p (c t)"), S1[:, 0:D], xnT_ready)

            def take_logits(g, i):
                act.wait_ge(lg_psum, g * TG + i + 1)
                copy(lg[:, i % J, i // J, :], S0[:, 0:E], lg_ready)

            def gelu(g, e, k):
                act.wait_ge(h_psum, 4 * (g * E + e) + k + 1)
                act.activation(hT[:, e % 2, 2 * k:2 * k + 2, :].rearrange("p f n -> p (f n)"), HB[k % 2][:, :], ACT.Gelu).then_inc(h_ready, 1)

            def take_y(g, e, pair):
                n = g * E + e
                act.wait_ge(y_psum, 2 * n + pair + 1)
                if e >= 2:
                    for beta in range(2):
                        act.wait_ge(y_moved[e % 2][beta], 16 * (g * (E // 2) + e // 2))
                copy(ys[:, e % 2, pair, :], YB[pair][:, 0:D], y_ready)

            def take_xin(g, b):
                for c in range(DC):
                    act.wait_ge(xin_psum, DC * (g * BG + b) + c + 1)
                    copy(xin[:, c, :, b, :], HB[c][:, :].rearrange("p (e s) -> p e s", e=E), xin_ready)

            def take_GT(g, b):
                for j in range(J):
                    act.wait_ge(gt_psum, J * (g * BG + b) + j + 1)
                    copy(GT[:, b, :, P * j:P * (j + 1)], YB[j][:, :].rearrange("p (e t) -> p e t", e=EP), gt_ready)

            def begin_experts(g):
                for b in range(BG):
                    take_xin(g, b)
                    if b > 0:
                        take_GT(g, b - 1)
                take_GT(g, BG - 1)

            def gate_exp(g):
                act.wait_ge(gstep, 3 * g + 2)
                act.activation(pe_[:, :, :, :].rearrange("p j b e -> p (j b e)"),
                               lgs[:, :, :, :].rearrange("p j b e -> p (j b e)"), ACT.Exp).then_inc(gexp_ready, 1)

            def slots(ga, gf):
                for s in range(TG):
                    if ga is not None and s + 1 < TG:
                        take_ctT(ga, s + 1)
                    if ga is not None and s > 0:
                        take_coT(ga, s - 1)
                    if gf is not None:
                        gelu(gf, s, 0)
                        gelu(gf, s, 1)
                    if ga is not None and s + 1 < TG:
                        take_kv(ga, s + 1)
                    if ga is not None:
                        exponentials(ga, s)
                    if ga is not None and s > 0:
                        round_xn(ga, s - 1)
                    if gf is not None and s > 0:
                        take_y(gf, s - 1, 0)
                    if gf is not None:
                        gelu(gf, s, 2)
                        gelu(gf, s, 3)
                    if ga is not None and s > 0:
                        take_xnT(ga, s - 1)
                    if gf is not None and s > 0:
                        take_y(gf, s - 1, 1)
                    if ga is not None and s > 0:
                        take_logits(ga, s - 1)
                if ga is not None:
                    take_coT(ga, TG - 1)
                if gf is not None:
                    take_y(gf, E - 1, 0)
                if ga is not None:
                    round_xn(ga, TG - 1)
                    take_xnT(ga, TG - 1)
                if gf is not None:
                    take_y(gf, E - 1, 1)
                if ga is not None:
                    take_logits(ga, TG - 1)
                    gate_exp(ga)

            def first_loads(g):
                for i in range(2):
                    act.dma_start(ct[:, i, :], c_t[bass.ds(g * TG + i, 1)].rearrange("o p c -> p (o c)")).then_inc(c_loaded[i], 16)
                for i in range(3):
                    act.dma_start(xt[:, i, :], x_t[bass.ds(g * TG + i, 1)].rearrange("o p c -> p (o c)")).then_inc(x_loaded[i], 16)

            act.wait_ge(setup_b, 5 * 16)
            act.activation(tanh_g[:, :], gates[:, :], ACT.Tanh).then_inc(gates_tanh, 1)
            take_ctT(0, 0)
            take_kv(0, 0)
            slots(0, None)
            with act.Fori(0, G - 1) as g:
                first_loads(g + 1)
                take_ctT(g + 1, 0)
                take_kv(g + 1, 0)
                begin_experts(g)
                slots(g + 1, g)
            begin_experts(G - 1)
            slots(None, G - 1)

        @block.tensor
        def _(pe):
            def transposes(dst, src, n):
                for c in range(n):
                    ins = pe.transpose(dst[:, P * c:P * (c + 1)], src[:, P * c:P * (c + 1)], ident[:, :])
                return ins

            def ctx_transposes(g, i):
                t = g * TG + i
                pe.wait_ge(c_loaded[i % 2], 16 * (g * (TG // 2) + i // 2) + 16)
                if i == 1 and not isinstance(g, int):
                    pe.wait_ge(posT_ready, g)
                elif i >= 3:
                    pe.wait_ge(lg_ready, t - 2)
                transposes(S0, ct[:, i % 2, :], DC).then_inc(ctT_psum, 1)

            def project_kv(g, i):
                t = g * TG + i
                pe.wait_ge(ctT_ready, t + 1)
                if not (isinstance(g, int) and g == 0 and i < 2):
                    pe.wait_ge(cov_done, t - 1)
                for c in range(DC):
                    pe.matmul(KV[i % 2][:, :], ctT[:, c, :], wkvT[:, c, :], start=(c == 0), stop=False)
                pe.matmul(KV[i % 2][:, :], ones_b[:, :], bias_b[:, 0:2 * D], start=False, stop=True).then_inc(kv_psum, 1)

            def co_transposes(g, i):
                t = g * TG + i
                pe.wait_ge(con_ready, t + 1)
                if i == 0 and not isinstance(g, int):
                    pe.wait_ge(work_ready, g)
                transposes(S1, con[:, :], DC).then_inc(coT_psum, 1)

            def project_out(g, i):
                pe.wait_ge(coT_ready, g * TG + i + 1)
                for c in range(DC):
                    pe.matmul(S0[:, 0:D], coT[:, c, :], woT[:, c, :], start=(c == 0), stop=False)
                pe.matmul(S0[:, 0:D], ones_b[:, :], bias_b[:, 2 * D:3 * D], start=False, stop=True).then_inc(wo_psum, 1)

            def xn_transposes(g, i):
                pe.wait_ge(xn_ready, g * TG + i + 1)
                transposes(S1, xn[:, i % 2, :], DC).then_inc(xnT_psum, 1)

            def logits(g, i):
                pe.wait_ge(xnT_ready, g * TG + i + 1)
                for c in range(DC):
                    ins = pe.matmul(S0[:, 0:E], xnT[:, c, :], gwT[:, c, :], start=(c == 0), stop=(c == DC - 1))
                ins.then_inc(lg_psum, 1)

            def hidden(g, e, k):
                n = g * E + e
                if k == 0:
                    pe.wait_ge(w1_loaded[e % 2], 16 * (g * (E // 2) + e // 2) + 16)
                if e == 0 and k < 2:
                    pe.wait_ge(xin_ready, DC * BG * (g + 1))
                else:
                    pe.wait_ge(h_ready, 4 * n + k - 1)
                for f in (2 * k, 2 * k + 1):
                    for c in range(DC):
                        ins = pe.matmul(HB[k % 2][:, D * (f % 2):D * (f % 2 + 1)], w1s[:, e % 2, c, P * f:P * (f + 1)],
                                        xin[:, c, e, :, :].rearrange("p b s -> p (b s)"), start=(c == 0), stop=(c == DC - 1))
                ins.then_inc(h_psum, 1)

            def outputs(g, e, pair):
                n = g * E + e
                if pair == 0:
                    pe.wait_ge(w2_loaded[e % 2], 16 * (g * (E // 2) + e // 2) + 16)
                    pe.wait_ge(h_ready, 4 * n + 4)
                if e == 0:
                    pe.wait_ge(gt_ready, J * BG * (g + 1))
                else:
                    pe.wait_ge(y_ready, 2 * (n - 1) + pair + 1)
                for f in range(FC):
                    ins = pe.matmul(YB[pair][:, 0:D], hT[:, e % 2, f, P * pair:P * (pair + 1)], w2s[:, e % 2, f, :],
                                    start=(f == 0), stop=(f == FC - 1))
                ins.then_inc(y_psum, 1)

            def gather(g, b):
                n = g * BG + b
                pe.wait_ge(sel_ready, n + 1)
                for c in range(DC):
                    if b > 0:
                        pe.wait_ge(xin_ready, DC * (n - 1) + c + 1)
                    parts = [(part, j) for part in (xnh, xnl) for j in range(J)]
                    for k, (part, j) in enumerate(parts):
                        ins = pe.matmul(HB[c][:, :], part[:, J * b + j, P * c:P * (c + 1)],
                                        Sel[:, b, j, :, :].rearrange("p e s -> p (e s)"), start=(k == 0), stop=(k == len(parts) - 1))
                    ins.then_inc(xin_psum, 1)

            def gate_transposes(g, b):
                n = g * BG + b
                pe.wait_ge(gs_ready, n + 1)
                for j in range(J):
                    if b > 0:
                        pe.wait_ge(gt_ready, J * (n - 1) + j + 1)
                    transposes(YB[j], Gs[:, b % 2, j, :, :].rearrange("p e s -> p (e s)"), EP).then_inc(gt_psum, 1)

            def begin_experts(g):
                for b in range(BG):
                    gather(g, b)
                    if b > 0:
                        gate_transposes(g, b - 1)
                gate_transposes(g, BG - 1)

            def combine(g, i):
                b, j = i // J, i % J
                if i == 0:
                    for moved in y_moved[0] + y_moved[1]:
                        pe.wait_ge(moved, 16 * (E // 2) * (g + 1))
                    pe.wait_ge(y_ready, 2 * E * (g + 1))
                if i >= 4:
                    pe.wait_ge(fin_ready, TG * g + i - 3)
                for ep in range(EP):
                    ins = pe.matmul(CB[i % 4][:, 0:D], GT[:, b, ep, P * j:P * (j + 1)], Y[:, b, ep, :],
                                    start=(ep == 0), stop=(ep == EP - 1))
                ins.then_inc(comb_psum, 1)

            def slots(ga, gf):
                for s in range(TG):
                    if ga is not None and s + 1 < TG:
                        ctx_transposes(ga, s + 1)
                    if ga is not None and s > 0:
                        co_transposes(ga, s - 1)
                    if gf is not None:
                        hidden(gf, s, 0)
                        hidden(gf, s, 1)
                    if ga is not None and s + 1 < TG:
                        project_kv(ga, s + 1)
                    if ga is not None and s > 0:
                        project_out(ga, s - 1)
                    if gf is not None and s > 0:
                        outputs(gf, s - 1, 0)
                    if gf is not None:
                        hidden(gf, s, 2)
                        hidden(gf, s, 3)
                    if ga is not None and s > 0:
                        xn_transposes(ga, s - 1)
                    if gf is not None and s > 0:
                        outputs(gf, s - 1, 1)
                    if ga is not None and s > 0:
                        logits(ga, s - 1)

            def end_attention(g, gf):
                co_transposes(g, TG - 1)
                project_out(g, TG - 1)
                if gf is not None:
                    outputs(gf, E - 1, 0)
                xn_transposes(g, TG - 1)
                if gf is not None:
                    outputs(gf, E - 1, 1)
                logits(g, TG - 1)
                pe.wait_ge(pr_ready, g + 1)
                for j in range(J):
                    ins = pe.transpose(S1[0:BG * E, P * j:P * (j + 1)], pr[:, j, :, :].rearrange("p b e -> p (b e)"), ident[:, :])
                ins.then_inc(prT_psum, 1)
                if gf is not None:
                    for i in range(TG):
                        combine(gf, i)

            def position_transposes(g):
                pe.wait_ge(posm_ready, g + 1)
                for j in range(J):
                    ins = pe.transpose(S0[:, P * j:P * (j + 1)], posm[:, P * j:P * (j + 1)], ident[:, :])
                ins.then_inc(posT_psum, 1)

            pe.wait_ge(ident_ready, 2)
            pe.wait_ge(setup_loaded, 7 * 16)
            for c in range(DC):
                cols = slice(P * c, P * (c + 1))
                for a in range(4):
                    ins = pe.transpose(bank[4 + 2 * c][:, P * a:P * (a + 1)], wrow[:, a, cols], ident[:, :])
                ins.then_inc(setup_t, 1)
                for a in range(2):
                    pe.transpose(bank[5 + 2 * c][:, P * a:P * (a + 1)], wrow[:, 4 + a, cols], ident[:, :])
                pe.transpose(bank[5 + 2 * c][:, D:D + E], gwrow[:, cols], ident[0:E, 0:E]).then_inc(setup_t, 1)
            ctx_transposes(0, 0)
            pe.wait_ge(setup_ev, 4)
            pe.wait_ge(bias_moved, 3 * 16)
            project_kv(0, 0)
            slots(0, None)
            end_attention(0, None)
            with pe.Fori(0, G - 1) as g:
                ctx_transposes(g + 1, 0)
                project_kv(g + 1, 0)
                position_transposes(g)
                begin_experts(g)
                slots(g + 1, g)
                end_attention(g + 1, g)
            position_transposes(G - 1)
            begin_experts(G - 1)
            slots(None, G - 1)
            for pair in range(2):
                outputs(G - 1, E - 1, pair)
            for i in range(TG):
                combine(G - 1, i)


_INS = ['x', 'ctx_1024', 'g_xattn', 'g_ffn', 'L0_xattn_W_kv', 'L0_xattn_b_kv', 'L0_xattn_W_out', 'L0_xattn_b_out',
        'L0_ffn_gate_w', 'L0_ffn_w1', 'L0_ffn_w2']
_OUTS = [((16, 256, 256), 'float32')]


def kernel(**inputs):
    import numpy as _np
    import concourse.bacc as _bacc
    from concourse import mybir as _mybir
    from concourse.bass_utils import run_bass_kernel_spmd as _run

    nc = _bacc.Bacc("TRN2", target_bir_lowering=False, num_devices=1)
    arrays, args = {}, []
    for name in _INS:
        a = _np.ascontiguousarray(inputs[name])
        arrays[f"in_{name}_dram"] = a
        args.append(nc.dram_tensor(f"in_{name}_dram", a.shape, _mybir.dt.from_np(a.dtype), kind="ExternalInput").ap())
    for i, (shape, dtype) in enumerate(_OUTS):
        dt = _mybir.dt.from_np(_np.dtype(dtype))
        args.append(nc.dram_tensor(f"out_{i}_dram", shape, dt, kind="ExternalOutput").ap())
    flamingo_gated_block_kernel(nc, *args)
    r = _run(nc, [arrays], core_ids=[0])
    got = tuple(r.results[0][f"out_{i}_dram"] for i in range(len(_OUTS)))
    return got[0]
```

```python
from contextlib import ExitStack

import concourse.bass as bass
from concourse import mybir


def flamingo_gated_block_kernel(nc, x, ctx_in, g_xattn, g_ffn, W_kv, b_kv, W_out, b_out, gate_w, w1, w2, out):
    fp32 = mybir.dt.float32
    bf16 = mybir.dt.bfloat16
    f32r = mybir.dt.float32r
    ALU = mybir.AluOpType
    ACT = mybir.ActivationFunctionType
    AX = mybir.AxisListType

    B, T, D = x.shape
    E, _, F = w1.shape
    P = 128
    H = 16
    DK = D // H
    CAP = 2 * T // E
    G = 4
    BG = B // G
    J = T // P
    TG = BG * J
    DC = D // P
    FC = F // P
    EP = E // 2
    HK, HC = 10, 11
    HP = H - min(HK, HC)
    BV = 2
    NR = TG + 2
    EPS = 1e-5
    assert 2 * CAP == P and TG == E and BG == 4

    x_t = x.rearrange("b (j p) c -> (b j) p c", p=P)
    c_t = ctx_in.rearrange("b (j p) c -> (b j) p c", p=P)
    o_t = out.rearrange("b (j p) c -> (b j) p c", p=P)
    x2_d = nc.dram_tensor("x2_scratch", [B * J, P, D], fp32).ap()
    Q = 4
    FQ = F // Q
    w1_q = w1.rearrange("e (c p) (q f) -> e q p c f", p=P, q=Q)
    w1x_d = nc.dram_tensor("w1_parts", [E * Q, P, 2, DC, FQ], fp32).ap()
    w2_d = w2.rearrange("e (f p) d -> e p f d", p=P)

    es = ExitStack()
    with es:
        def sb(name, shape, dt=fp32):
            return es.enter_context(nc.sbuf_tensor(name, shape, dt))

        def sb_overlaid(first, second):
            with nc.sbuf_tensor(*first) as one:
                pass
            return one, sb(*second)

        def sem(name):
            return es.enter_context(nc.semaphore(name))

        def sems(name, k):
            return [sem(f"{name}{i}") for i in range(k)]

        ident = sb("ident", [P, P])
        minus_ident = sb("minus_ident", [P, P], f32r)
        iota1 = sb("iota1", [P, CAP])
        ones_f = sb("ones_f", [P, T])
        ones_b = sb("ones_b", [3, P], bf16)
        neg_half = sb("neg_half", [P, 2])
        tanh_g = sb("tanh_g", [P, 2])
        gates = sb("gates", [P, 2])
        wkvT = sb("wkvT", [P, DC, 2 * D])
        woT = sb("woT", [P, DC, D])
        gwT = sb("gwT", [P, DC, E])
        bias_b = sb("bias_b", [3, 3 * D], bf16)

        xt = sb("xt", [P, 4, D])
        ct = sb("ct", [P, 2, D])
        ctT = sb("ctT", [P, DC, P])
        q = sb("q", [P, 2, D])
        kvs = sb("kvs", [P, 2, 2 * D])
        hp1, prod_v = sb_overlaid(("hp1", [P, max(HK, HC) * DK * DK], f32r), ("prod_v", [P, max(HK, HC) * DK * DK], fp32))
        prod_p = sb("prod_p", [P, HP * DK * DK])
        wrow = prod_v[:, 0:6 * D].rearrange("p (a c) -> p a c", c=D)
        bias_row = prod_v[0:1, 6 * D:9 * D]
        gwrow = prod_v[0:E, 9 * D:10 * D]
        bias_pc = prod_p[0:1, :].bitcast(bf16)[:, 0:9 * D].rearrange("o (k n) -> o k n", k=3)
        tree_a = sb("tree_a", [P, HP * DK * 8])
        tree_b = sb("tree_b", [P, HP * DK * 4])
        tree_c = sb("tree_c", [P, HP * DK * 2])
        S = sb("S", [P, H * DK])
        Sc = sb("Sc", [P, H * DK])
        mx = sb("mx", [P, H])
        Ex = sb("Ex", [P, H * DK])
        den = sb("den", [P, H])
        rden = sb("rden", [P, H])
        co = sb("co", [P, D])
        con = sb("con", [P, D])
        coT = sb("coT", [P, DC, P])
        x2 = sb("x2", [P, 2, D])
        st1 = sb("st1", [P, 6])
        st2 = sb("st2", [P, 6])
        mv = sb("mv", [P, 2, 2])
        ve = sb("ve", [P, 2])
        rs = sb("rs", [P, 2])
        xn = sb("xn", [P, 2, D])
        xnh = sb("xnh", [P, TG, D], f32r)
        xnl = sb("xnl", [P, TG, D], f32r)
        xnT = sb("xnT", [P, DC, P])

        lg = sb("lg", [P, J, BG, E])
        lgs = sb("lgs", [P, J, BG, E])
        gmx = sb("gmx", [P, J * BG])
        pe_ = sb("pe_", [P, J, BG, E])
        gsum = sb("gsum", [P, J * BG])
        grec = sb("grec", [P, J * BG])
        pr = sb("pr", [P, J, BG, E])
        work, mask, cum = (prod_v[0:BG * E, T * k:T * (k + 1)] for k in range(3))
        top8 = sb("top8", [BG * E, 8])
        spare = sb("spare", [P, 1])
        posm = sb("posm", [P, T])
        posT = sb("posT", [P, J, BG, E])
        Sel, hT = sb_overlaid(("Sel", [P, BG, J, E, CAP], f32r), ("hT", [P, 2, FC, BG * CAP], fp32))

        xin = sb("xin", [P, 2, DC, E, BG, CAP], f32r)
        GT = sb("GT", [P, BG, EP, T])
        w1in, w1s = sb_overlaid(("w1in", [P, Q, 2, DC, FQ], fp32), ("w1s", [P, Q, 2, DC, FQ], f32r))
        w2l, w2s = sb_overlaid(("w2l", [P, 2, FC, D], f32r), ("w2s", [P, 2, FC, D], fp32))
        w2h = xnh
        hh = [xnl[:, :, :], hp1[:, 0:FC * BG * CAP].rearrange("p (f n) -> p f n", f=FC)]
        hl = Sel[:, :, :, :, :].rearrange("p (x y) j e s -> p x (y j e s)", x=2).rearrange("p x (f n) -> p x f n", f=FC)
        ys = sb("ys", [P, 2, 2, D])
        Y = sb("Y", [P, BG, EP, D])
        Gs = Y[:, :, :, :].rearrange("p b e t -> p b (e t)").rearrange("p b (j e s) -> p b j e s", j=J, e=E)
        w1raw = Y
        xr = sb("xr", [P, 4, D])

        bank = [es.enter_context(nc.psum_tensor(f"bank{i}", [P, 512], fp32)) for i in range(8)]
        KV, S0, S1, HB, YB = bank[0:2], bank[2], bank[3], bank[4:6], bank[6:8]
        XB = HB + [S1]
        CB = HB + YB

        rest_loaded = sem("rest_loaded")
        setup_loaded, setup_b, gates_loaded, gates_tanh = sem("setup_loaded"), sem("setup_b"), sem("gates_loaded"), sem("gates_tanh")
        ident_ready, consts_ready = sem("ident_ready"), sem("consts_ready")
        setup_t, setup_ev = sem("setup_t"), sem("setup_ev")
        bias_rows, bias_step, bias_moved = sem("bias_rows"), sem("bias_step"), sem("bias_moved")
        mv_set, grec_ready = sem("mv_set"), sem("grec_ready")
        x_loaded, c_loaded = sems("x_loaded", 4), sems("c_loaded", 2)
        ctT_psum, ctT_ready, kv_psum, kvs_ready = sem("ctT_psum"), sem("ctT_ready"), sem("kv_psum"), sem("kvs_ready")
        st_x, st_x2, mv_ready, ve_ready, rs_ready = sem("st_x"), sem("st_x2"), sem("mv_ready"), sem("ve_ready"), sem("rs_ready")
        q_ready, xn_ready = sem("q_ready"), sem("xn_ready")
        xnh_ready, xnl_ready = sem("xnh_ready"), sem("xnl_ready")
        prodv_s, prodp_s, tree_s = sem("prodv_s"), sem("prodp_s"), sem("tree_s")
        Sv_done, Sp_done, mx_done, Sc_ready, E_ready, den_done, rden_done = (
            sem("Sv_done"), sem("Sp_done"), sem("mx_done"), sem("Sc_ready"), sem("E_ready"), sem("den_done"), sem("rden_done"))
        cov_done, cop_done, con_ready = sem("cov_done"), sem("cop_done"), sem("con_ready")
        coT_psum, coT_ready, wo_psum, x2_ready, x2_stored = (
            sem("coT_psum"), sem("coT_ready"), sem("wo_psum"), sem("x2_ready"), sems("x2_stored", 2))
        xnT_psum, xnT_ready, lg_psum, lg_ready = sem("xnT_psum"), sem("xnT_ready"), sem("lg_psum"), sem("lg_ready")
        gstep, gexp_ready, pr_ready, prT_psum, work_ready, found8, removed8, mask_ready, cum_ready, posm_ready = (
            sem("gstep"), sem("gexp_ready"), sem("pr_ready"), sem("prT_psum"), sem("work_ready"), sem("found8"),
            sem("removed8"), sem("mask_ready"), sem("cum_ready"), sem("posm_ready"))
        posT_psum, posT_ready, sel_ready = sem("posT_psum"), sem("posT_ready"), sem("sel_ready")
        w2h_ready, w2l_ready, hh_ready, hl_ready = sem("w2h_ready"), sem("w2l_ready"), sem("hh_ready"), sem("hl_ready")
        gs_ready, gsv_ready = sem("gs_ready"), sem("gsv_ready")
        gt_psum, gt_ready, xin_psum, xin_ready = sem("gt_psum"), sem("gt_ready"), sem("xin_psum"), sem("xin_ready")
        w1_loaded, w2_loaded = sems("w1_loaded", Q), sems("w2_loaded", 2)
        raw_loaded, high_made, low_psum, low_made, parts_stored = (
            sems("raw_loaded", Q), sem("high_made"), sem("low_psum"), sem("low_made"), sems("parts_stored", Q))
        minus_ready, w1_ready = sem("minus_ready"), sem("w1_ready")
        h_psum, h_ready, y_psum, y_ready = sem("h_psum"), sem("h_ready"), sem("y_psum"), sem("y_ready")
        y_moved = [sems("y_moved_even", 2), sems("y_moved_odd", 2)]
        comb_psum, fin_ready = sem("comb_psum"), sem("fin_ready")
        xr_loaded, out_stored = sems("xr_loaded", 4), sems("out_stored", 4)
        out_done = sem("out_done")

        block = es.enter_context(nc.Block())

        @block.sync
        def _(sp):
            def load_x(g, i):
                t = g * TG + i
                if not (isinstance(g, int) and g == 0 and i < 4):
                    sp.wait_ge(x2_ready, t - 3)
                sp.dma_start(xt[:, i % 4, :], x_t[bass.ds(t, 1)].rearrange("o p c -> p (o c)")).then_inc(x_loaded[i % 4], 16)

            def load_c(g, i):
                t = g * TG + i
                if not (isinstance(g, int) and g == 0 and i < 2):
                    sp.wait_ge(ctT_psum, t - 1)
                sp.dma_start(ct[:, i % 2, :], c_t[bass.ds(t, 1)].rearrange("o p c -> p (o c)")).then_inc(c_loaded[i % 2], 16)

            def store_x2(g, i, known=False):
                t = g * TG + i
                if not known:
                    sp.wait_ge(x2_ready, t + 1)
                sp.dma_start(x2_d[bass.ds(t, 1)].rearrange("o p c -> p (o c)"), x2[:, i % 2, :]).then_inc(x2_stored[i % 2], 16)

            def load_w1(g, e, k):
                if not (isinstance(g, int) and g == 0 and e == 0):
                    sp.wait_ge(h_psum, Q * (g * E + e - 1) + k + 1)
                sp.dma_start(w1in[:, k], w1x_d[Q * (e % E) + k]).then_inc(w1_loaded[k], 16)

            def load_raw(e, k):
                if e > 0:
                    sp.wait_ge(low_psum, Q * (e - 1) + k + 1)
                sp.dma_start(w1raw[:, k, 0:DC, :], w1_q[e, k]).then_inc(raw_loaded[k], 16)

            def store_parts(e, k):
                sp.wait_ge(low_made, Q * e + k + 1)
                sp.dma_start(w1x_d[Q * e + k], w1s[:, k].bitcast(fp32)).then_inc(parts_stored[k], 16)

            def load_w2(g, e):
                if not (isinstance(g, int) and g == 0 and e < 2):
                    sp.wait_ge(y_psum, 2 * (g * E + e - 1))
                sp.dma_start(w2s[:, e % 2, :, :], w2_d[e % E]).then_inc(w2_loaded[e % 2], 16)

            def move_y(g, e):
                n = g * E + e
                sp.wait_ge(y_ready, 2 * n + 2)
                for beta in range(2):
                    rows = slice(CAP * (e % 2), CAP * (e % 2) + CAP)
                    sp.dma_start(Y[rows, beta:BG:2, e // 2, :], ys[CAP * beta:CAP * beta + CAP, e % 2, :, :]).then_inc(y_moved[e % 2][beta], 16)

            def load_xr(g, i):
                if i >= 4:
                    sp.wait_ge(out_stored[i % 4], 16 * (g + 1))
                sp.dma_start(xr[:, i % 4, :], x2_d[bass.ds(g * TG + i, 1)].rearrange("o p c -> p (o c)")).then_inc(xr_loaded[i % 4], 16)

            def finish(g):
                for i in range(TG):
                    store_out(g, i)
                    if i + 4 < TG:
                        load_xr(g, i + 4)
                sp.wait_ge(out_done, 16 * (TG - 4) * (g + 1))

            def store_out(g, i):
                t = g * TG + i
                sp.wait_ge(fin_ready, t + 1)
                sp.dma_start(o_t[bass.ds(t, 1)].rearrange("o p c -> p (o c)"), xr[:, i % 4, :]).then_inc(out_stored[i] if i < 4 else out_done, 16)

            sp.dma_start(con[0:1, 0:D], b_kv.rearrange("(o a n) -> o a n", o=1, a=2)[:, 0, :]).then_inc(setup_b, 16)
            sp.dma_start(co[0:1, 0:D], b_kv.rearrange("(o a n) -> o a n", o=1, a=2)[:, 1, :]).then_inc(setup_b, 16)
            sp.dma_start(bias_row[0:1, 2 * D:3 * D], b_out.rearrange("(o n) -> o n", o=1)).then_inc(setup_b, 16)
            sp.dma_start(ct[:, 0, :], c_t[0]).then_inc(c_loaded[0], 16)
            for a in range(DC):
                sp.dma_start(wrow[:, 4 + a, :], W_out[P * a:P * (a + 1), :]).then_inc(rest_loaded, 16)
            sp.dma_start(gwrow[:, :], gate_w).then_inc(rest_loaded, 16)
            sp.dma_start(xt[:, 0, :], x_t[0]).then_inc(x_loaded[0], 16)
            sp.dma_start(gates[:, 0:1], g_xattn.rearrange("(a n) -> a n", a=1).broadcast_to([P, 1])).then_inc(gates_loaded, 16)
            sp.dma_start(gates[:, 1:2], g_ffn.rearrange("(a n) -> a n", a=1).broadcast_to([P, 1])).then_inc(gates_loaded, 16)
            load_x(0, 1)
            load_c(0, 1)
            sp.wait_ge(bias_step, 5)
            for k in range(3):
                sp.dma_start(bias_b[k:k + 1, :], bias_pc[0:1, k, :]).then_inc(bias_moved, 16)
            load_x(0, 2)
            for k in range(Q):
                load_raw(0, k)
            for e in range(2):
                load_w2(0, e)

            def slot_loads(g, i):
                if i + 3 < TG:
                    load_x(g, i + 3)
                if i + 2 < TG:
                    load_c(g, i + 2)

            for i in range(TG):
                slot_loads(0, i)
                for k in range(Q):
                    store_parts(i, k)
                    if i + 1 < E:
                        load_raw(i + 1, k)
                if i > 0:
                    store_x2(0, i - 1)
            for stored in parts_stored:
                sp.wait_ge(stored, 16 * E)
            for k in range(Q):
                load_w1(0, 0, k)
            store_x2(0, TG - 1)
            with sp.Fori(0, G - 1) as g:
                for s in range(TG):
                    slot_loads(g + 1, s)
                    for k in range(2):
                        load_w1(g, s + 1, k)
                    if s > 0:
                        store_x2(g + 1, s - 1)
                    for k in range(2, Q):
                        load_w1(g, s + 1, k)
                    if s > 0:
                        load_w2(g, s + 1)
                        move_y(g, s - 1)
                for i in range(4):
                    load_xr(g, i)
                move_y(g, E - 1)
                load_w2(g, E + 1)
                finish(g)
                store_x2(g + 1, TG - 1, known=True)
            for s in range(E):
                if s + 1 < E:
                    for k in range(Q):
                        load_w1(G - 1, s + 1, k)
                if s > 0:
                    if s + 1 < E:
                        load_w2(G - 1, s + 1)
                    move_y(G - 1, s - 1)
            for stored in x2_stored:
                sp.wait_ge(stored, 16 * B * J // 2)
            for i in range(4):
                load_xr(G - 1, i)
            move_y(G - 1, E - 1)
            finish(G - 1)

        @block.gpsimd
        def _(pool):
            def share(heads, in0, in1, dst, n_tree, done):
                full = [P, heads, DK, DK]
                in0, in1 = in0.unsqueeze(1).broadcast_to(full), in1.unsqueeze(2).broadcast_to(full)
                pv = prod_p[:, 0:heads * DK * DK].rearrange("p (h a b) -> p h a b", a=DK, b=DK)
                pool.tensor_tensor(pv, in0, in1, ALU.mult).then_inc(prodp_s, 1)
                pool.wait_ge(prodp_s, n_tree + 1)
                src = prod_p[:, 0:heads * DK * DK].rearrange("p (r b) -> p r b", b=DK)
                for k, buf in enumerate((tree_a, tree_b, tree_c)):
                    w = DK >> (k + 1)
                    nxt = buf[:, 0:heads * DK * w].rearrange("p (r b) -> p r b", b=w)
                    pool.tensor_tensor(nxt, src[:, :, 0:w], src[:, :, w:2 * w], ALU.add).then_inc(tree_s, 1)
                    pool.wait_ge(tree_s, 3 * n_tree + k + 1)
                    src = nxt
                pool.tensor_tensor(dst.rearrange("p (r b) -> p r b", b=1), src[:, :, 0:1], src[:, :, 1:2], ALU.add).then_inc(done, 1)

            def rsqrt(n):
                pool.wait_ge(ve_ready, n + 1)
                pool.tensor_tensor(rs[:, :], ve[:, :], neg_half[:, :], ALU.pow).then_inc(rs_ready, 1)

            def tile_of(g, i):
                t = g * TG + i
                qi = q[:, i % 2, :].rearrange("p (h d) -> p h d", d=DK)[:, HK:H, :]
                Kv = kvs[:, i % 2, 0:D].rearrange("p (t d) -> p t d", d=DK)
                Vv = kvs[:, i % 2, D:2 * D].rearrange("p (d t) -> p d t", t=DK)
                Ev = Ex[:, :].rearrange("p (h t) -> p h t", t=DK)[:, HC:H, :]
                pool.wait_ge(q_ready, t + 1)
                pool.wait_ge(kvs_ready, t + 1)
                if not (isinstance(g, int) and g == 0 and i == 0):
                    pool.wait_ge(Sc_ready, t)
                share(H - HK, Kv, qi, S[:, HK * DK:H * DK], 2 * t, Sp_done)
                rsqrt(NR * g + i + 1)
                pool.wait_ge(E_ready, t + 1)
                if not (isinstance(g, int) and g == 0 and i == 0):
                    pool.wait_ge(con_ready, t)
                share(H - HC, Vv, Ev, co[:, HC * DK:H * DK], 2 * t + 1, cop_done)

            def low_xn(g, i):
                pool.wait_ge(xnh_ready, g * TG + i + 1)
                pool.tensor_tensor(xnl[:, i, :], xn[:, i % 2, :], xnh[:, i, :].bitcast(fp32), ALU.subtract).then_inc(xnl_ready, 1)

            def attention(g):
                for i in range(TG):
                    tile_of(g, i)
                    if i > 0:
                        low_xn(g, i - 1)
                rsqrt(NR * g + TG + 1)
                low_xn(g, TG - 1)

            def gated_selection(g):
                for b in range(BG - BV):
                    pool.wait_ge(sel_ready, g * BG + b + 1)
                    for j in range(J):
                        ins = pool.tensor_tensor(Gs[:, b, j], Sel[:, b, j].bitcast(fp32), pr[:, j, b, :].unsqueeze(2).broadcast_to([P, E, CAP]), ALU.mult)
                    ins.then_inc(gs_ready, 1)

            pool.iota(iota1[:, :], pattern=[[1, CAP]], base=1, channel_multiplier=0,
                      allow_small_or_imprecise_dtypes=True).then_inc(consts_ready, 1)
            pool.memset(neg_half[:, :], -0.5).then_inc(consts_ready, 1)
            pool.memset(ident[:, :], 0.0).then_inc(ident_ready, 1)
            pool.wait_ge(ident_ready, 1)
            pool.affine_select(out=ident[:, :], in_=ident[:, :], compare_op=ALU.not_equal, fill=1.0,
                               base=0, pattern=[[-1, P]], channel_multiplier=1).then_inc(ident_ready, 1)
            pool.wait_ge(ident_ready, 2)
            pool.tensor_scalar(minus_ident[:, :], ident[:, :], -1.0, None, ALU.mult).then_inc(minus_ready, 1)
            pool.wait_ge(consts_ready, 2)
            rsqrt(0)
            attention(0)
            with pool.Fori(0, G - 1) as g:
                gated_selection(g)
                rsqrt(NR * (g + 1))
                attention(g + 1)
            gated_selection(G - 1)

        @block.vector
        def _(dve):
            def first(g, i=0):
                return isinstance(g, int) and g == 0 and i == 0

            def wait_apart(sem, value):
                dve.wait_ge(sem, value)
                dve.memset(spare[:, :], 0.0)

            def products(heads, in0, in1, dst, n, done):
                full = [P, heads, DK, DK]
                in0, in1 = in0.unsqueeze(1).broadcast_to(full), in1.unsqueeze(2).broadcast_to(full)
                pv = prod_v[:, 0:heads * DK * DK].rearrange("p (h a b) -> p h a b", a=DK, b=DK)
                dve.tensor_tensor(pv, in0, in1, ALU.mult).then_inc(prodv_s, 1)
                dve.wait_ge(prodv_s, n + 1)
                dve.tensor_reduce(dst, prod_v[:, 0:heads * DK * DK].rearrange("p (r b) -> p r b", b=DK), axis=AX.X, op=ALU.add).then_inc(done, 1)

            def stats(g, i_x, i_x2):
                if i_x is not None:
                    t = g * TG + i_x
                    dve.wait_ge(x_loaded[i_x % 4], 16 * (g * (TG // 4) + i_x // 4) + 16)
                    dve.bn_stats(st1[:, :], xt[:, i_x % 4, :]).then_inc(st_x, 1)
                    wait_apart(st_x, t + 1)
                    dve.bn_aggr(mv[:, 0, :], st1[:, :]).then_inc(mv_ready, 1)
                if i_x2 is not None:
                    t = g * TG + i_x2
                    dve.wait_ge(x2_ready, t + 1)
                    dve.bn_stats(st2[:, :], x2[:, i_x2 % 2, :]).then_inc(st_x2, 1)
                    wait_apart(st_x2, t + 1)
                    dve.bn_aggr(mv[:, 1, :], st2[:, :]).then_inc(mv_ready, 1)
                done = (TG if i_x is None else i_x + 1) + (0 if i_x2 is None else i_x2 + 1)
                dve.wait_ge(mv_ready, 2 * TG * g + done)
                dve.tensor_scalar(ve[:, :], mv[:, :, 1], EPS, None, ALU.add).then_inc(ve_ready, 1)

            def make_q(g, i):
                dve.tensor_scalar(q[:, i % 2, :], xt[:, i % 4, :], mv[:, 0, 0:1], rs[:, 0:1], ALU.subtract, ALU.mult).then_inc(q_ready, 1)

            def make_xn(g, i):
                if i == 0:
                    dve.wait_ge(xin_psum, 2 * DC * BG * g)
                dve.tensor_scalar(xn[:, i % 2, :], x2[:, i % 2, :], mv[:, 1, 0:1], rs[:, 1:2], ALU.subtract, ALU.mult).then_inc(xn_ready, 1)

            def residual(g, i):
                t = g * TG + i
                dve.wait_ge(wo_psum, t + 1)
                if not (isinstance(g, int) and g == 0 and i < 2):
                    dve.wait_ge(x2_stored[i % 2], 16 * (g * (TG // 2) + i // 2))
                dve.scalar_tensor_tensor(x2[:, i % 2, :], S0[:, 0:D], tanh_g[:, 0:1], xt[:, i % 4, :],
                                         ALU.mult, ALU.add).then_inc(x2_ready, 1)

            def tile_of(g, i):
                t = g * TG + i
                kvp = KV[i % 2]
                Kp = kvp[:, 0:D].rearrange("p (t d) -> p t d", d=DK)
                Vp = kvp[:, D:2 * D].rearrange("p (d t) -> p d t", t=DK)
                qi = q[:, i % 2, :].rearrange("p (h d) -> p h d", d=DK)[:, 0:HK, :]
                Ev = Ex[:, :].rearrange("p (h t) -> p h t", t=DK)
                dve.wait_ge(kvs_ready, t + 1)
                dve.wait_ge(q_ready, t + 1)
                products(HK, Kp, qi, S[:, 0:HK * DK], 2 * t, Sv_done)
                if i > 0:
                    residual(g, i - 1)
                stats(g, i + 1 if i + 1 < TG else None, i - 1 if i > 0 else None)
                dve.wait_ge(Sp_done, t + 1)
                dve.wait_ge(Sv_done, t + 1)
                Sv = S[:, :].rearrange("p (h t) -> p h t", t=DK)
                dve.reduce_max(mx[:, :], Sv, AX.X).then_inc(mx_done, 1)
                dve.wait_ge(mx_done, t + 1)
                if not first(g, i):
                    dve.wait_ge(E_ready, t)
                dve.tensor_tensor(Sc[:, :].rearrange("p (h t) -> p h t", t=DK), Sv,
                                  mx[:, :].unsqueeze(2).broadcast_to([P, H, DK]), ALU.subtract).then_inc(Sc_ready, 1)
                dve.wait_ge(rs_ready, NR * g + i + 2)
                if i + 1 < TG:
                    if not (isinstance(g, int) and g == 0 and i == 0):
                        dve.wait_ge(cop_done, t)
                    make_q(g, i + 1)
                if i > 0:
                    make_xn(g, i - 1)
                dve.wait_ge(E_ready, t + 1)
                dve.tensor_reduce(den[:, :], Ev, axis=AX.X, op=ALU.add).then_inc(den_done, 1)
                products(HC, Vp, Ev[:, 0:HC, :], co[:, 0:HC * DK], 2 * t + 1, cov_done)
                dve.wait_ge(den_done, t + 1)
                dve.reciprocal(rden[:, :], den[:, :]).then_inc(rden_done, 1)
                dve.wait_ge(rden_done, t + 1)
                dve.wait_ge(cop_done, t + 1)
                dve.wait_ge(cov_done, t + 1)
                if not first(g, i):
                    dve.wait_ge(coT_psum, t)
                dve.tensor_tensor(con[:, :].rearrange("p (h d) -> p h d", d=DK), co[:, :].rearrange("p (h d) -> p h d", d=DK),
                                  rden[:, :].unsqueeze(2).broadcast_to([P, H, DK]), ALU.mult).then_inc(con_ready, 1)

            def first_q(g):
                dve.wait_ge(rs_ready, NR * g + 1)
                make_q(g, 0)

            def end_attention(g):
                residual(g, TG - 1)
                stats(g, None, TG - 1)
                dve.wait_ge(rs_ready, NR * g + NR)
                make_xn(g, TG - 1)

            def gate_softmax(g):
                v8 = lambda m: m[:, :, :, :].rearrange("p j b e -> p (j b) e")
                bc = lambda m: m[:, :].unsqueeze(2).broadcast_to([P, J * BG, E])
                dve.wait_ge(lg_ready, TG * g + TG)
                dve.reduce_max(gmx[:, :], v8(lg), AX.X).then_inc(gstep, 1)
                dve.wait_ge(gstep, 3 * g + 1)
                dve.tensor_tensor(v8(lgs), v8(lg), bc(gmx), ALU.subtract).then_inc(gstep, 1)
                dve.wait_ge(gexp_ready, g + 1)
                dve.reduce_sum(gsum[:, :], v8(pe_), AX.X).then_inc(gstep, 1)
                dve.wait_ge(gstep, 3 * g + 3)
                dve.reciprocal(grec[:, :], gsum[:, :]).then_inc(grec_ready, 1)
                dve.wait_ge(grec_ready, g + 1)
                dve.tensor_tensor(v8(pr), v8(pe_), bc(grec), ALU.mult).then_inc(pr_ready, 1)

            sums_after = {4: 0, 6: 1}

            def choose_tokens(g, gl):
                dve.wait_ge(prT_psum, g + 1)
                dve.tensor_copy(work[:, :], S1[0:BG * E, 0:T]).then_inc(work_ready, 1)
                wait_apart(work_ready, g + 1)
                for r in range(CAP // 8):
                    n = g * (CAP // 8) + r
                    dve.max(top8[:, :], work[:, :]).then_inc(found8, 1)
                    wait_apart(found8, n + 1)
                    dve.match_replace(work[:, :], top8[:, :], work[:, :], -1.0).then_inc(removed8, 1)
                    if gl is not None and r in sums_after:
                        last_sum(gl, sums_after[r])
                    wait_apart(removed8, n + 1)
                dve.tensor_scalar(mask[:, :], work[:, :], 0.0, None, ALU.is_lt).then_inc(mask_ready, 1)
                dve.wait_ge(mask_ready, g + 1)
                dve.tensor_tensor_scan(cum[:, :], ones_f[0:BG * E, :], mask[:, :], 0.0, ALU.mult, ALU.add).then_inc(cum_ready, 1)
                dve.wait_ge(cum_ready, g + 1)
                dve.tensor_tensor(posm[0:BG * E, :], cum[:, :], mask[:, :], ALU.mult).then_inc(posm_ready, 1)
                if gl is not None:
                    last_sum(gl, 2)
                    last_sum(gl, 3)

            def last_sum(g, i):
                dve.wait_ge(comb_psum, g * TG + i + 1)
                dve.wait_ge(xr_loaded[i % 4], 16 * (g * (TG // 4) + i // 4) + 16)
                dve.scalar_tensor_tensor(xr[:, i % 4, :], CB[i % 4][:, 0:D], tanh_g[:, 1:2], xr[:, i % 4, :],
                                         ALU.mult, ALU.add).then_inc(fin_ready, 1)

            def selection(g, gl):
                dve.wait_ge(posT_psum, g + 1)
                dve.tensor_copy(posT[:, :, :, :].rearrange("p j b e -> p j (b e)"),
                                S0[:, 0:T].rearrange("p (j n) -> p j n", j=J)[:, :, 0:BG * E]).then_inc(posT_ready, 1)
                dve.wait_ge(posT_ready, g + 1)
                for b in range(BG):
                    if b % 2 == 0 and b > 0 and gl is not None:
                        last_sum(gl, 4)
                        last_sum(gl, 5)
                    for j in range(J):
                        ins = dve.tensor_tensor(Sel[:, b, j], iota1[:, :].unsqueeze(1).broadcast_to([P, E, CAP]),
                                                posT[:, j, b, :].unsqueeze(2).broadcast_to([P, E, CAP]), ALU.is_equal)
                    ins.then_inc(sel_ready, 1)
                if gl is not None:
                    last_sum(gl, 6)
                    last_sum(gl, 7)

            def gated_selection(g):
                dve.wait_ge(sel_ready, BG * (g + 1))
                for b in range(BG - BV, BG):
                    for j in range(J):
                        ins = dve.tensor_tensor(Gs[:, b, j], Sel[:, b, j].bitcast(fp32), pr[:, j, b, :].unsqueeze(2).broadcast_to([P, E, CAP]), ALU.mult)
                    ins.then_inc(gsv_ready, 1)

            def take_GT(g):
                for b in range(BG):
                    for j in range(J):
                        dve.wait_ge(gt_psum, J * (g * BG + b) + j + 1)
                        dve.tensor_copy(GT[:, b, :, P * j:P * (j + 1)], YB[j][:, :].rearrange("p (e t) -> p e t", e=EP)).then_inc(gt_ready, 1)

            def split_experts(g):
                for e in range(E + 1):
                    if e > 0:
                        x = (e - 1) % 2
                        dve.wait_ge(w2_loaded[x], 16 * (g * (E // 2) + (e - 1) // 2) + 16)
                        if e > 1:
                            dve.wait_ge(y_psum, 2 * (g * E + e - 1))
                        for k in range(2):
                            fs = slice(FC // 2 * k, FC // 2 * (k + 1))
                            dve.tensor_copy(w2h[:, fs, :], w2s[:, x, fs, :]).then_inc(w2h_ready, 1)
                            dve.wait_ge(w2h_ready, 2 * (e - 1) + k + 1)
                            dve.tensor_tensor(w2l[:, x, fs, :], w2s[:, x, fs, :], w2h[:, fs, :].bitcast(fp32), ALU.subtract).then_inc(w2l_ready, 1)
                    if e < E:
                        for k in range(Q):
                            fs = slice(FC // Q * k, FC // Q * (k + 1))
                            dve.wait_ge(h_ready, Q * (g * E + e) + k + 1)
                            dve.tensor_copy(hh[e % 2][:, fs, :], hT[:, e % 2, fs, :]).then_inc(hh_ready, 1)
                            dve.wait_ge(hh_ready, Q * e + k + 1)
                            dve.tensor_tensor(hl[:, e % 2, fs, :], hT[:, e % 2, fs, :], hh[e % 2][:, fs, :].bitcast(fp32), ALU.subtract).then_inc(hl_ready, 1)

            dve.memset(ones_f[:, :], 1.0).then_inc(consts_ready, 1)
            dve.memset(ones_b[:, :], 1.0).then_inc(consts_ready, 1)
            dve.memset(posm[:, :], 0.0).then_inc(consts_ready, 1)
            dve.wait_ge(setup_b, 3 * 16)
            for half, row in enumerate((con, co)):
                src = row[0:1, 0:D].rearrange("o (t d two) -> o two t d", d=DK, two=2)
                hk = H // 2
                dve.tensor_copy(bias_row[0:1, D // 2 * half:D // 2 * (half + 1)].rearrange("o (t d) -> o t d", d=DK), src[:, 0])
                dve.tensor_copy(bias_row[0:1, D:2 * D].rearrange("o (d t) -> o t d", t=H)[:, hk * half:hk * (half + 1), :], src[:, 1]).then_inc(bias_rows, 1)
            dve.wait_ge(bias_rows, 2)
            for k in range(3):
                dve.tensor_copy(bias_pc[0:1, k, :], bias_row[0:1, :]).then_inc(bias_step, 1)
                dve.wait_ge(bias_step, 2 * k + 1)
                if k < 2:
                    dve.tensor_tensor(bias_row[0:1, :], bias_row[0:1, :], bias_pc[0:1, k, :], ALU.subtract).then_inc(bias_step, 1)
                    dve.wait_ge(bias_step, 2 * k + 2)
            dve.memset(mv[:, 1, :], 1.0).then_inc(mv_set, 1)
            dve.wait_ge(mv_set, 1)
            stats(0, 0, None)
            first_q(0)
            dve.wait_ge(gates_tanh, 1)

            for i in range(TG):
                tile_of(0, i)
            end_attention(0)
            gate_softmax(0)
            choose_tokens(0, None)
            selection(0, None)
            with dve.Fori(0, G - 1) as g:
                stats(g + 1, 0, None)
                gated_selection(g)
                first_q(g + 1)
                for i in range(TG):
                    tile_of(g + 1, i)
                end_attention(g + 1)
                gate_softmax(g + 1)
                choose_tokens(g + 1, g)
                selection(g + 1, g)
            gated_selection(G - 1)
            take_GT(G - 1)
            split_experts(G - 1)
            for i in range(TG):
                last_sum(G - 1, i)

        @block.scalar
        def _(act):
            def copy(dst, src, done):
                act.activation(dst, src, ACT.Copy).then_inc(done, 1)

            def take_ctT(g, i):
                act.wait_ge(ctT_psum, g * TG + i + 1)
                copy(ctT[:, :, :].rearrange("p c t -> p (c t)"), S0[:, 0:D], ctT_ready)

            def take_kv(g, i):
                t = g * TG + i
                act.wait_ge(kv_psum, t + 1)
                if not (isinstance(g, int) and g == 0 and i < 2):
                    act.wait_ge(cop_done, t - 1)
                copy(kvs[:, i % 2, :], KV[i % 2][:, :], kvs_ready)

            def exponentials(g, i):
                t = g * TG + i
                act.wait_ge(Sc_ready, t + 1)
                if not (isinstance(g, int) and g == 0 and i == 0):
                    act.wait_ge(cov_done, t)
                    act.wait_ge(cop_done, t)
                act.activation(Ex[:, :], Sc[:, :], ACT.Exp, scale=DK ** -0.5).then_inc(E_ready, 1)

            def take_coT(g, i):
                act.wait_ge(coT_psum, g * TG + i + 1)
                copy(coT[:, :, :].rearrange("p c t -> p (c t)"), S1[:, 0:D], coT_ready)

            def round_xn(g, i):
                act.wait_ge(xn_ready, g * TG + i + 1)
                copy(xnh[:, i, :], xn[:, i % 2, :], xnh_ready)

            def take_xnT(g, i):
                act.wait_ge(xnT_psum, g * TG + i + 1)
                copy(xnT[:, :, :].rearrange("p c t -> p (c t)"), S1[:, 0:D], xnT_ready)

            def take_logits(g, i):
                act.wait_ge(lg_psum, g * TG + i + 1)
                copy(lg[:, i % J, i // J, :], S1[:, D:D + E], lg_ready)

            def gelu(g, e, k):
                act.wait_ge(h_psum, Q * (g * E + e) + k + 1)
                if e < 2 and k == 0:
                    act.wait_ge(gs_ready, (BG - BV) * (g + 1))
                    act.wait_ge(gsv_ready, BV * (g + 1))
                act.activation(hT[:, e % 2, 2 * k:2 * k + 2, :].rearrange("p f n -> p (f n)"), HB[k % 2][:, :], ACT.Gelu).then_inc(h_ready, 1)

            def take_y(g, e, pair):
                n = g * E + e
                act.wait_ge(y_psum, 2 * n + pair + 1)
                if e >= 2:
                    for beta in range(2):
                        act.wait_ge(y_moved[e % 2][beta], 16 * (g * (E // 2) + e // 2))
                copy(ys[:, e % 2, pair, :], YB[pair][:, 0:D], y_ready)

            def take_xin(g, b):
                for m in range(2 * DC):
                    act.wait_ge(xin_psum, 2 * DC * (g * BG + b) + m + 1)
                    copy(xin[:, m // DC, m % DC, :, b, :], XB[(2 * DC * b + m) % 3][:, :].rearrange("p (e s) -> p e s", e=E), xin_ready)

            def type_w1(g, e, k):
                n = g * E + e
                act.wait_ge(w1_loaded[k], 16 * (n + 1))
                copy(w1s[:, k], w1in[:, k], w1_ready)

            def make_high(e, k):
                act.wait_ge(raw_loaded[k], 16 * (e + 1))
                if e > 0:
                    act.wait_ge(parts_stored[k], 16 * e)
                copy(w1s[:, k, 0], w1raw[:, k, 0:DC, :], high_made)

            def take_low(e, k):
                act.wait_ge(low_psum, Q * e + k + 1)
                copy(w1s[:, k, 1], CB[k][:, :].rearrange("p (c f) -> p c f", c=DC), low_made)

            def split_w1(e, ks):
                for k in ks:
                    make_high(e, k)
                for k in ks:
                    take_low(e, k)

            def take_GT(g, b):
                for j in range(J):
                    act.wait_ge(gt_psum, J * (g * BG + b) + j + 1)
                    copy(GT[:, b, :, P * j:P * (j + 1)], YB[j][:, :].rearrange("p (e t) -> p e t", e=EP), gt_ready)

            def begin_experts(g):
                for b in range(BG):
                    take_xin(g, b)
                    if b > 0 and not isinstance(g, int):
                        take_GT(g, b - 1)

            def gate_exp(g):
                act.wait_ge(gstep, 3 * g + 2)
                act.activation(pe_[:, :, :, :].rearrange("p j b e -> p (j b e)"),
                               lgs[:, :, :, :].rearrange("p j b e -> p (j b e)"), ACT.Exp).then_inc(gexp_ready, 1)

            def slots(ga, gf):
                for s in range(TG):
                    if ga is not None and s + 1 < TG:
                        take_ctT(ga, s + 1)
                    if gf is not None and s == 0:
                        type_w1(gf, 0, 2)
                        type_w1(gf, 0, 3)
                        if ga is not None:
                            exponentials(ga, 0)
                    if gf is not None:
                        gelu(gf, s, 0)
                        gelu(gf, s, 1)
                        if s == 0 and ga is not None:
                            take_GT(gf, BG - 1)
                        if s > 0:
                            type_w1(gf, s, 2)
                    if ga is not None and s > 0:
                        take_coT(ga, s - 1)
                    if ga is not None and s + 1 < TG:
                        take_kv(ga, s + 1)
                    if gf is not None and s > 0:
                        type_w1(gf, s, 3)
                    if gf is None:
                        split_w1(s, (0, 1))
                    if ga is not None and (gf is None or s > 0):
                        exponentials(ga, s)
                    if gf is None:
                        split_w1(s, (2, 3))
                    if ga is not None and s > 0:
                        round_xn(ga, s - 1)
                    if gf is not None and s > 0:
                        take_y(gf, s - 1, 0)
                    if gf is not None:
                        gelu(gf, s, 2)
                        gelu(gf, s, 3)
                        if ga is not None or s + 1 < E:
                            type_w1(gf, s + 1, 0)
                    if ga is not None and s > 0:
                        take_xnT(ga, s - 1)
                    if gf is not None and s > 0:
                        take_y(gf, s - 1, 1)
                    if ga is not None and s > 0:
                        take_logits(ga, s - 1)
                    if gf is not None and (ga is not None or s + 1 < E):
                        type_w1(gf, s + 1, 1)
                if ga is not None:
                    take_coT(ga, TG - 1)
                if gf is not None:
                    take_y(gf, E - 1, 0)
                if ga is not None:
                    round_xn(ga, TG - 1)
                    take_xnT(ga, TG - 1)
                    take_logits(ga, TG - 1)
                    gate_exp(ga)
                if gf is not None:
                    take_y(gf, E - 1, 1)

            def first_loads(g):
                for i in range(2):
                    act.dma_start(ct[:, i, :], c_t[bass.ds(g * TG + i, 1)].rearrange("o p c -> p (o c)")).then_inc(c_loaded[i], 16)
                for i in range(3):
                    act.dma_start(xt[:, i, :], x_t[bass.ds(g * TG + i, 1)].rearrange("o p c -> p (o c)")).then_inc(x_loaded[i], 16)

            for a in range(DC):
                rows = W_kv[2 * P * a:2 * P * (a + 1), :].rearrange("(n two) c -> two n c", two=2)
                for kv in range(2):
                    act.dma_start(wrow[:, 2 * kv + a, :], rows[kv]).then_inc(setup_loaded, 16)
            take_ctT(0, 0)
            for c in range(DC):
                act.wait_ge(setup_t, c + 1)
                src = bank[4 + 2 * c]
                act.activation(wkvT[:, c, 0:D], src[:, 0:D], ACT.Copy)
                act.activation(wkvT[:, c, D:2 * D].rearrange("p (d t) -> p t d", t=H),
                               src[:, D:2 * D].rearrange("p (t d) -> p t d", d=DK), ACT.Copy).then_inc(setup_ev, 1)
            for c in range(DC):
                act.wait_ge(setup_t, DC + c + 1)
                src = bank[5 + 2 * c]
                act.activation(woT[:, c, :], src[:, 0:D], ACT.Copy)
                act.activation(gwT[:, c, :], src[:, D:D + E], ACT.Copy).then_inc(setup_ev, 1)
            act.wait_ge(gates_loaded, 2 * 16)
            act.activation(tanh_g[:, :], gates[:, :], ACT.Tanh).then_inc(gates_tanh, 1)
            take_kv(0, 0)
            slots(0, None)
            for k in range(2):
                type_w1(0, 0, k)
            with act.Fori(0, G - 1) as g:
                first_loads(g + 1)
                take_ctT(g + 1, 0)
                take_kv(g + 1, 0)
                begin_experts(g)
                slots(g + 1, g)
            begin_experts(G - 1)
            slots(None, G - 1)

        @block.tensor
        def _(pe):
            def transposes(dst, src, n):
                for c in range(n):
                    ins = pe.transpose(dst[:, P * c:P * (c + 1)], src[:, P * c:P * (c + 1)], ident[:, :])
                return ins

            def ctx_transposes(g, i):
                t = g * TG + i
                pe.wait_ge(c_loaded[i % 2], 16 * (g * (TG // 2) + i // 2) + 16)
                if i == 0 and not isinstance(g, int):
                    pe.wait_ge(posT_ready, g)
                transposes(S0, ct[:, i % 2, :], DC).then_inc(ctT_psum, 1)

            def project_kv(g, i):
                t = g * TG + i
                pe.wait_ge(ctT_ready, t + 1)
                if not (isinstance(g, int) and g == 0 and i < 2):
                    pe.wait_ge(cov_done, t - 1)
                for c in range(DC):
                    pe.matmul(KV[i % 2][:, :], ctT[:, c, :], wkvT[:, c, :], start=(c == 0), stop=False)
                if isinstance(g, int) and i == 0:
                    pe.wait_ge(bias_moved, 3 * 16)
                pe.matmul(KV[i % 2][:, :], ones_b[:, :], bias_b[:, 0:2 * D], start=False, stop=True).then_inc(kv_psum, 1)

            def co_transposes(g, i):
                t = g * TG + i
                pe.wait_ge(con_ready, t + 1)
                if i == 0 and not isinstance(g, int):
                    pe.wait_ge(work_ready, g)
                if i > 0:
                    pe.wait_ge(lg_ready, t)
                transposes(S1, con[:, :], DC).then_inc(coT_psum, 1)

            def project_out(g, i):
                pe.wait_ge(coT_ready, g * TG + i + 1)
                for c in range(DC):
                    pe.matmul(S0[:, 0:D], coT[:, c, :], woT[:, c, :], start=(c == 0), stop=False)
                pe.matmul(S0[:, 0:D], ones_b[:, :], bias_b[:, 2 * D:3 * D], start=False, stop=True).then_inc(wo_psum, 1)

            def xn_transposes(g, i):
                pe.wait_ge(xn_ready, g * TG + i + 1)
                transposes(S1, xn[:, i % 2, :], DC).then_inc(xnT_psum, 1)

            def logits(g, i):
                pe.wait_ge(xnT_ready, g * TG + i + 1)
                for c in range(DC):
                    ins = pe.matmul(S1[:, D:D + E], xnT[:, c, :], gwT[:, c, :], start=(c == 0), stop=(c == DC - 1))
                ins.then_inc(lg_psum, 1)

            def hidden(g, e, k):
                n = g * E + e
                pe.wait_ge(w1_ready, Q * n + k + 1)
                if e == 0 and k < 2:
                    pe.wait_ge(xin_ready, 2 * DC * BG * (g + 1))
                else:
                    pe.wait_ge(h_ready, 4 * n + k - 1)
                terms = [(c, w, x_) for c in range(DC) for w, x_ in ((0, 0), (0, 1), (1, 0))]
                for f in range(2):
                    for m, (c, w, x_) in enumerate(terms):
                        ins = pe.matmul(HB[k % 2][:, D * f:D * (f + 1)], w1s[:, k, w, c, P * f:P * (f + 1)],
                                        xin[:, x_, c, e, :, :].rearrange("p b s -> p (b s)"), start=(m == 0), stop=(m == len(terms) - 1))
                ins.then_inc(h_psum, 1)

            def outputs(g, e, pair):
                n = g * E + e
                last = isinstance(g, int)
                if pair == 0 and not last:
                    pe.wait_ge(w2_loaded[e % 2], 16 * (g * (E // 2) + e // 2) + 16)
                    pe.wait_ge(h_ready, 4 * n + 4)
                if pair == 0 and last:
                    pe.wait_ge(hl_ready, Q * (e + 1))
                if e == 0:
                    pe.wait_ge(gt_ready, J * BG * (g + 1))
                else:
                    pe.wait_ge(y_ready, 2 * (n - 1) + pair + 1)
                cols = slice(P * pair, P * (pair + 1))
                for f in range(FC):
                    if not last:
                        ins = pe.matmul(YB[pair][:, 0:D], hT[:, e % 2, f, cols], w2s[:, e % 2, f, :],
                                        start=(f == 0), stop=(f == FC - 1))
                        continue
                    if pair == 0 and f % (FC // 2) == 0:
                        pe.wait_ge(w2l_ready, 2 * e + f // (FC // 2) + 1)
                    pe.matmul(YB[pair][:, 0:D], hh[e % 2][:, f, cols], w2h[:, f, :], start=(f == 0), stop=False)
                    pe.matmul(YB[pair][:, 0:D], hh[e % 2][:, f, cols], w2l[:, e % 2, f, :], start=False, stop=False)
                    ins = pe.matmul(YB[pair][:, 0:D], hl[:, e % 2, f, cols], w2h[:, f, :], start=False, stop=(f == FC - 1))
                ins.then_inc(y_psum, 1)

            def gather(g, b):
                n = g * BG + b
                if b == 0:
                    pe.wait_ge(xnl_ready, TG * (g + 1))
                pe.wait_ge(sel_ready, g * BG + max(b, 2) + 1)
                for m in range(2 * DC):
                    if b > 0 or m >= 3:
                        pe.wait_ge(xin_ready, 2 * DC * n + m - 2)
                    part, c = (xnh, xnl)[m // DC], m % DC
                    for j in range(J):
                        ins = pe.matmul(XB[(2 * DC * b + m) % 3][:, :], part[:, J * b + j, P * c:P * (c + 1)],
                                        Sel[:, b, j, :, :].rearrange("p e s -> p (e s)"), start=(j == 0), stop=(j == J - 1))
                    ins.then_inc(xin_psum, 1)

            def gate_transposes(g, b):
                n = g * BG + b
                if b == 0:
                    pe.wait_ge(gsv_ready, BV * g + 1)
                if b < BG - BV:
                    pe.wait_ge(gs_ready, (BG - BV) * g + b + 1)
                else:
                    pe.wait_ge(gsv_ready, BV * g + b - (BG - BV) + 1)
                for j in range(J):
                    if b > 0:
                        pe.wait_ge(gt_ready, J * (n - 1) + j + 1)
                    transposes(YB[j], Gs[:, b, j, :, :].rearrange("p e s -> p (e s)"), EP).then_inc(gt_psum, 1)

            def begin_experts(g):
                for b in range(BG):
                    gather(g, b)
                    if b > 0:
                        gate_transposes(g, b - 1)

            def combine(g, i, pairs=range(EP)):
                b, j = i // J, i % J
                if i == 0:
                    for moved in y_moved[0] + y_moved[1]:
                        pe.wait_ge(moved, 16 * ((E // 2) * g + pairs[-1] + 1))
                if i == 2:
                    pe.wait_ge(y_ready, 2 * E * (g + 1))
                if i >= 4:
                    pe.wait_ge(fin_ready, TG * g + i - 3)
                for ep in pairs:
                    ins = pe.matmul(CB[i % 4][:, 0:D], GT[:, b, ep, P * j:P * (j + 1)], Y[:, b, ep, :],
                                    start=(ep == 0), stop=(ep == EP - 1))
                if ep == EP - 1:
                    ins.then_inc(comb_psum, 1)

            def low_part(e, k):
                pe.wait_ge(high_made, Q * e + k + 1)
                if e > 0:
                    pe.wait_ge(low_made, Q * (e - 1) + k + 1)
                pe.matmul(CB[k][:, :], ident[:, :], w1raw[:, k, 0:DC, :].rearrange("p c f -> p (c f)"), start=True, stop=False)
                pe.matmul(CB[k][:, :], minus_ident[:, :], w1s[:, k, 0].rearrange("p c f -> p (c f)"),
                          start=False, stop=True).then_inc(low_psum, 1)

            def begin_combine(g):
                for i in range(2):
                    combine(g, i, range(0, EP - 1))
                for i in range(2):
                    combine(g, i, range(EP - 1, EP))

            def slots(ga, gf):
                for s in range(TG):
                    if ga is not None and s + 1 < TG:
                        ctx_transposes(ga, s + 1)
                    if gf is not None:
                        hidden(gf, s, 0)
                        hidden(gf, s, 1)
                        if s == 0:
                            gate_transposes(gf, BG - 1)
                    if ga is not None and s > 0:
                        co_transposes(ga, s - 1)
                    if ga is not None and s + 1 < TG:
                        project_kv(ga, s + 1)
                    if ga is not None and s > 0:
                        project_out(ga, s - 1)
                    if gf is None:
                        for k in range(Q):
                            low_part(s, k)
                    if gf is not None and s > 0:
                        outputs(gf, s - 1, 0)
                    if gf is not None:
                        hidden(gf, s, 2)
                        hidden(gf, s, 3)
                    if ga is not None and s > 0:
                        xn_transposes(ga, s - 1)
                    if gf is not None and s > 0:
                        outputs(gf, s - 1, 1)
                    if ga is not None and s > 0:
                        logits(ga, s - 1)

            def end_attention(g, gf):
                co_transposes(g, TG - 1)
                project_out(g, TG - 1)
                if gf is not None:
                    outputs(gf, E - 1, 0)
                xn_transposes(g, TG - 1)
                logits(g, TG - 1)
                if gf is not None:
                    outputs(gf, E - 1, 1)
                pe.wait_ge(pr_ready, g + 1)
                for j in range(J):
                    ins = pe.transpose(S1[0:BG * E, P * j:P * (j + 1)], pr[:, j, :, :].rearrange("p b e -> p (b e)"), ident[:, :])
                ins.then_inc(prT_psum, 1)
                if gf is not None:
                    begin_combine(gf)
                    for i in range(2, 6):
                        combine(gf, i)
                position_transposes(g)
                if gf is not None:
                    for i in range(6, TG):
                        combine(gf, i)

            def position_transposes(g):
                pe.wait_ge(posm_ready, g + 1)
                for j in range(J):
                    ins = pe.transpose(S0[:, P * j:P * (j + 1)], posm[:, P * j:P * (j + 1)], ident[:, :])
                ins.then_inc(posT_psum, 1)

            pe.wait_ge(ident_ready, 2)
            ctx_transposes(0, 0)
            pe.wait_ge(setup_loaded, 4 * 16)
            for c in range(DC):
                for a in range(4):
                    ins = pe.transpose(bank[4 + 2 * c][:, P * a:P * (a + 1)], wrow[:, a, P * c:P * (c + 1)], ident[:, :])
                ins.then_inc(setup_t, 1)
            pe.wait_ge(rest_loaded, 3 * 16)
            for c in range(DC):
                cols = slice(P * c, P * (c + 1))
                for a in range(2):
                    pe.transpose(bank[5 + 2 * c][:, P * a:P * (a + 1)], wrow[:, 4 + a, cols], ident[:, :])
                pe.transpose(bank[5 + 2 * c][:, D:D + E], gwrow[:, cols], ident[0:E, 0:E]).then_inc(setup_t, 1)
            pe.wait_ge(setup_ev, DC)
            project_kv(0, 0)
            pe.wait_ge(setup_ev, 2 * DC)
            pe.wait_ge(minus_ready, 1)
            slots(0, None)
            end_attention(0, None)
            with pe.Fori(0, G - 1) as g:
                ctx_transposes(g + 1, 0)
                project_kv(g + 1, 0)
                begin_experts(g)
                slots(g + 1, g)
                end_attention(g + 1, g)
            begin_experts(G - 1)
            slots(None, G - 1)
            for pair in range(2):
                outputs(G - 1, E - 1, pair)
            begin_combine(G - 1)
            for i in range(2, TG):
                combine(G - 1, i)


_INS = ['x', 'ctx_1024', 'g_xattn', 'g_ffn', 'L0_xattn_W_kv', 'L0_xattn_b_kv', 'L0_xattn_W_out', 'L0_xattn_b_out',
        'L0_ffn_gate_w', 'L0_ffn_w1', 'L0_ffn_w2']
_OUTS = [((16, 256, 256), 'float32')]


def kernel(**inputs):
    import numpy as _np
    import concourse.bacc as _bacc
    from concourse import mybir as _mybir
    from concourse.bass_utils import run_bass_kernel_spmd as _run

    nc = _bacc.Bacc("TRN2", target_bir_lowering=False, num_devices=1)
    arrays, args = {}, []
    for name in _INS:
        a = _np.ascontiguousarray(inputs[name])
        arrays[f"in_{name}_dram"] = a
        args.append(nc.dram_tensor(f"in_{name}_dram", a.shape, _mybir.dt.from_np(a.dtype), kind="ExternalInput").ap())
    for i, (shape, dtype) in enumerate(_OUTS):
        dt = _mybir.dt.from_np(_np.dtype(dtype))
        args.append(nc.dram_tensor(f"out_{i}_dram", shape, dt, kind="ExternalOutput").ap())
    flamingo_gated_block_kernel(nc, *args)
    r = _run(nc, [arrays], core_ids=[0])
    got = tuple(r.results[0][f"out_{i}_dram"] for i in range(len(_OUTS)))
    return got[0]
```
